# Optimizing a Trainium2 kernel written in Bass

```python
import numpy as np
import jax
import jax.numpy as jnp

def _softmax(x, axis=-1):
    return jax.nn.softmax(x, axis=axis)

def _gelu(x):
    return jax.nn.gelu(x, approximate=True)

def _silu(x):
    return jax.nn.silu(x)

def _sigmoid(x):
    return jax.nn.sigmoid(x)

def _layernorm(x, axis=-1, eps=1e-05):
    m = jnp.mean(x, axis=axis, keepdims=True)
    v = jnp.var(x, axis=axis, keepdims=True)
    return (x - m) / jnp.sqrt(v + eps)

def _scatter_add(tgt, idx, src, axis=0):
    return tgt.at[idx].add(src)

def _segment_sum(src, seg, n):
    return jax.ops.segment_sum(src, seg, n)
kernel_name = 'mk_adj_resnorm_d2_adj_r2_90fb25'

def setup_inputs(seed: int=0):
    np.random.seed(seed)
    _w = jnp.asarray

    def _rec_inputs():
        import jax
        import jax.numpy as jnp
        _gk = jax.random.key(seed)
        x = -0.000125 + 0.9999 * jax.random.normal(jax.random.fold_in(_gk, 1), (64, 128, 128), jnp.float32)
        _a = jax.random.bernoulli(jax.random.fold_in(_gk, 2), 0.0625, (128, 128))
        _a = jnp.logical_or(_a, jnp.swapaxes(_a, -1, -2))
        _a = jnp.logical_or(_a, jnp.eye(128, dtype=bool))
        _af = _a.astype(jnp.float32)
        _af = _af * jax.random.uniform(jax.random.fold_in(_gk, 3), (128, 128), jnp.float32, 0.05, 0.000488281)
        adj = _af
        return (x, adj)
    x, adj = _rec_inputs()

    def _L0_gnn_setup():
        import jax, jax.numpy as jnp
        import numpy as np
        B, T, D, H = (64, 1024, 128, 128)
        MAX_SKIP = 4

        def _lstm_last(Wih, Whh, bih, bhh, xs):
            N, _, Hd = xs.shape
            bias = bih + bhh

            def step(carry, x_t):
                h, c = carry
                g = x_t @ Wih.T + h @ Whh.T + bias
                i, f, gg, o = jnp.split(g, 4, axis=-1)
                c = jax.nn.sigmoid(f) * c + jax.nn.sigmoid(i) * jnp.tanh(gg)
                h = jax.nn.sigmoid(o) * jnp.tanh(c)
                return ((h, c), None)
            init = (jnp.zeros((N, Hd), xs.dtype), jnp.zeros((N, Hd), xs.dtype))
            (h_last, _), _ = jax.lax.scan(step, init, jnp.swapaxes(xs, 0, 1))
            return h_last
        key = jax.random.key(seed)
        ks = jax.random.split(key, 8)
        s = 0.05
        x = jax.random.normal(ks[0], (B, T, D), jnp.float32)
        adj = jax.random.uniform(ks[1], (T, T), jnp.float32) / T
        Wg0 = jax.random.normal(ks[2], (D, H), jnp.float32) * s
        bg0 = jnp.zeros((H,), jnp.float32)
        Wg1 = jax.random.normal(ks[3], (H, H), jnp.float32) * s
        bg1 = jnp.zeros((H,), jnp.float32)
        Wih = jax.random.normal(ks[4], (MAX_SKIP, 4 * H, H), jnp.float32) * s
        Whh = jax.random.normal(ks[5], (MAX_SKIP, 4 * H, H), jnp.float32) * s
        bih = jax.random.normal(ks[6], (MAX_SKIP, 4 * H), jnp.float32) * s
        bhh = jax.random.normal(ks[7], (MAX_SKIP, 4 * H), jnp.float32) * s
        return dict(x=x, adj=adj, Wg0=Wg0, bg0=bg0, Wg1=Wg1, bg1=bg1, Wih=Wih, Whh=Whh, bih=bih, bhh=bhh)
    _L0_gnn_all = _L0_gnn_setup()
    _L0_gnn_in = {k: v for k, v in _L0_gnn_all.items() if k in ('Wg0', 'bg0', 'Wg1', 'bg1', 'Wih', 'Whh', 'bih', 'bhh')}
    del _L0_gnn_all

    def _L1_gnn_setup():
        import jax, jax.numpy as jnp
        import numpy as np
        B, N, IN_DIM, OUT_DIM, H = (2, 2048, 128, 128, 4)
        HEAD_DIM = OUT_DIM // H
        EDGE_P = 0.01
        key = jax.random.key(seed)
        k1, k2, k3 = jax.random.split(key, 3)
        h = jax.random.normal(k1, (B, N, IN_DIM), dtype=jnp.float32)
        W = jax.random.normal(k2, (IN_DIM, 3 * OUT_DIM), dtype=jnp.float32) / np.sqrt(IN_DIM)
        adj = (jax.random.uniform(k3, (N, N)) < EDGE_P).astype(jnp.float32)
        adj = jnp.maximum(adj, jnp.eye(N, dtype=jnp.float32))
        return {'h': h, 'W': W, 'adj': adj}
    _L1_gnn_all = _L1_gnn_setup()
    _L1_gnn_in = {k: v for k, v in _L1_gnn_all.items() if k in ('W',)}
    del _L1_gnn_all
    return {'x': x, 'adj': adj, 'L0_gnn_Wg0': _L0_gnn_in['Wg0'], 'L0_gnn_bg0': _L0_gnn_in['bg0'], 'L0_gnn_Wg1': _L0_gnn_in['Wg1'], 'L0_gnn_bg1': _L0_gnn_in['bg1'], 'L0_gnn_Wih': _L0_gnn_in['Wih'], 'L0_gnn_Whh': _L0_gnn_in['Whh'], 'L0_gnn_bih': _L0_gnn_in['bih'], 'L0_gnn_bhh': _L0_gnn_in['bhh'], 'L1_gnn_W': _L1_gnn_in['W']}

def reference(x, adj, L0_gnn_Wg0, L0_gnn_bg0, L0_gnn_Wg1, L0_gnn_bg1, L0_gnn_Wih, L0_gnn_Whh, L0_gnn_bih, L0_gnn_bhh, L1_gnn_W):
    import jax
    import jax.numpy as jnp

    def _L0_gnn_ref(x, adj, Wg0, bg0, Wg1, bg1, Wih, Whh, bih, bhh):
        import jax, jax.numpy as jnp
        import numpy as np
        B, T, D, H = (64, 1024, 128, 128)
        MAX_SKIP = 4

        def _lstm_last(Wih, Whh, bih, bhh, xs):
            N, _, Hd = xs.shape
            bias = bih + bhh

            def step(carry, x_t):
                h, c = carry
                g = x_t @ Wih.T + h @ Whh.T + bias
                i, f, gg, o = jnp.split(g, 4, axis=-1)
                c = jax.nn.sigmoid(f) * c + jax.nn.sigmoid(i) * jnp.tanh(gg)
                h = jax.nn.sigmoid(o) * jnp.tanh(c)
                return ((h, c), None)
            init = (jnp.zeros((N, Hd), xs.dtype), jnp.zeros((N, Hd), xs.dtype))
            (h_last, _), _ = jax.lax.scan(step, init, jnp.swapaxes(xs, 0, 1))
            return h_last
        h = jax.nn.relu(jnp.einsum('ts,bsh->bth', adj, x @ Wg0 + bg0))
        h = jax.nn.relu(jnp.einsum('ts,bsh->bth', adj, h @ Wg1 + bg1))
        Bv, Tv, Hd = h.shape
        for p in range(1, MAX_SKIP + 1):
            nw = Tv // p
            wins = h[:, :nw * p, :].reshape(Bv * nw, p, Hd)
            last = _lstm_last(Wih[p - 1], Whh[p - 1], bih[p - 1], bhh[p - 1], wins)
            idx = jnp.arange(nw) * p + (p - 1)
            h = h.at[:, idx, :].set(last.reshape(Bv, nw, Hd))
        return h

    def _L1_gnn_ref(h, W, adj):
        import jax, jax.numpy as jnp
        import numpy as np
        B, N, IN_DIM, OUT_DIM, H = (2, 2048, 128, 128, 4)
        HEAD_DIM = OUT_DIM // H
        EDGE_P = 0.01
        Bn, Nn, _ = h.shape
        qkv = h @ W
        qkv = qkv.reshape(Bn, Nn, 3, H, HEAD_DIM).transpose(2, 0, 3, 1, 4)
        q, k, v = (qkv[0], qkv[1], qkv[2])
        mask = jnp.where(adj == 0, -jnp.inf, 0.0)
        scores = jnp.einsum('bhid,bhjd->bhij', q, k) / np.sqrt(HEAD_DIM) + mask
        attn = jax.nn.softmax(scores, axis=-1)
        out = jnp.einsum('bhij,bhjd->bhid', attn, v)
        return out.transpose(0, 2, 1, 3).reshape(Bn, Nn, OUT_DIM)
    x = _layernorm(x + _L0_gnn_ref(x, adj, L0_gnn_Wg0, L0_gnn_bg0, L0_gnn_Wg1, L0_gnn_bg1, L0_gnn_Wih, L0_gnn_Whh, L0_gnn_bih, L0_gnn_bhh), axis=-1)
    x = _layernorm(x + _L1_gnn_ref(x, L1_gnn_W, adj), axis=-1)
    return x

_drawn_inputs = setup_inputs


def setup_inputs(seed=0):
    import zlib

    import numpy as np

    out = dict(_drawn_inputs(seed))
    spreads = {'L0_gnn_bg0': (0.0, 0.8), 'L0_gnn_bg1': (0.0, 0.8)}
    factors = {'L0_gnn_Wg0': 8.0, 'L0_gnn_Wg1': 8.0, 'L0_gnn_Wih': 7.588, 'L0_gnn_Whh': 8.0}
    for name, (base, spread) in spreads.items():
        noise = np.random.default_rng([zlib.crc32(name.encode()), seed]).standard_normal(out[name].shape)
        drawn = base * np.exp(spread * noise) if base else spread * noise
        out[name] = jnp.asarray(drawn.astype(out[name].dtype))
    for name, factor in factors.items():
        out[name] = (out[name] * factor).astype(out[name].dtype)
    return out
```

```python
from contextlib import ExitStack

import concourse.bass as bass
from concourse import mybir

ALU = mybir.AluOpType
ACT = mybir.ActivationFunctionType
AX_X = mybir.AxisListType.X
F32 = mybir.dt.float32
F32R = mybir.dt.float32r
BF16 = mybir.dt.bfloat16

BATCH, STEPS, DIM = 64, 128, 128
P = 128
GB = 4
GROUPS = BATCH // GB
HEADS = 4
HEAD_DIM = DIM // HEADS
MAX_SKIP = 4
EPS = 1e-5
MASKED = -1e30
QUARTERS = (0, 1, 2, 3)
GATE_I, GATE_F, GATE_G, GATE_O = QUARTERS
GATE_FUNCTION = {GATE_I: ACT.Sigmoid, GATE_F: ACT.Sigmoid, GATE_G: ACT.Tanh, GATE_O: ACT.Sigmoid}

WINDOWS = {p: STEPS // p for p in range(1, MAX_SKIP + 1)}
CHUNK = {1: 8, 2: 8, 3: 7, 4: 8}
PAIRS = {p: WINDOWS[p] // CHUNK[p] // 2 for p in CHUNK}
assert all(PAIRS[p] * 2 * CHUNK[p] == WINDOWS[p] for p in CHUNK)


def gates_of(step):
    return (GATE_I, GATE_G, GATE_O) if step == 0 else (GATE_I, GATE_G, GATE_F, GATE_O)


class Jobs:

    def __init__(self, p, jobs_before, gates_before, later_before):
        self.p, self.jobs0, self.gates0, self.later0 = p, jobs_before, gates_before, later_before
        self.jobs_per_pair = 2 * p
        self.gates_per_pair = 2 * (3 + 4 * (p - 1))
        self.later_per_pair = 2 * (p - 1)

    def job(self, pair, step, side):
        return pair * self.jobs_per_pair + (self.jobs0 + 2 * step + side)

    def gates(self, pair, step, side):
        own = 3 * side if step == 0 else 6 + 8 * (step - 1) + 4 * side
        return pair * self.gates_per_pair + (self.gates0 + own)

    def later(self, pair, step, side):
        return pair * self.later_per_pair + (self.later0 + 2 * (step - 1) + side)

    def after(self):
        return (self.job(PAIRS[self.p], 0, 0), self.gates(PAIRS[self.p], 0, 0),
                PAIRS[self.p] * self.later_per_pair + self.later0)


JOBS = {}
_counts = (0, 0, 0)
for _p in range(1, MAX_SKIP + 1):
    JOBS[_p] = Jobs(_p, *_counts)
    _counts = JOBS[_p].after()
ALL_JOBS = _counts[0]


def gates_before_last(p, step, side):
    if side == 1:
        return len(gates_of(step))
    return len(gates_of(step - 1 if step > 0 else p - 1))


def reach(engine, semaphore, count):
    if not isinstance(count, int) or count > 0:
        engine.wait_ge(semaphore, count)


def build(nc, x, adj, Wg0, bg0, Wg1, bg1, Wih, Whh, bih, bhh, Wqkv, out):
    x_groups = x.rearrange("(g b) t d -> g t b d", b=GB)
    out_groups = out.rearrange("(g b) t d -> g t b d", b=GB)

    with ExitStack() as ctx:
        def sem(name):
            return ctx.enter_context(nc.semaphore(name))

        def sb(stack, name, shape, dtype=F32):
            return stack.enter_context(nc.sbuf_tensor(name, shape, dtype))

        bank = ctx.enter_context(nc.psum_tensor("bank", [P, 8, 512], F32))

        ident = sb(ctx, "ident", [P, P])
        ident_bf = sb(ctx, "ident_bf", [P, P], BF16)
        mask = sb(ctx, "mask", [P, 1, P], BF16)
        wqkv = sb(ctx, "wqkv", [P, 3 * DIM])
        xr = [sb(ctx, f"xr{q}", [P, GB, DIM]) for q in range(2)]
        state = sb(ctx, "state", [P, STEPS, BATCH])

        lstm_mem = ExitStack()
        state_hi = sb(lstm_mem, "state_hi", [P, STEPS, BATCH], F32R)
        state_lo = sb(lstm_mem, "state_lo", [P, STEPS, BATCH], F32R)
        wih_hi = sb(lstm_mem, "wih_hi", [P, MAX_SKIP, 4, P], F32R)
        wih_lo = sb(lstm_mem, "wih_lo", [P, MAX_SKIP, 4, P], F32R)
        whh_hi = sb(lstm_mem, "whh_hi", [P, MAX_SKIP, 4, P], F32R)
        whh_lo = sb(lstm_mem, "whh_lo", [P, MAX_SKIP, 4, P], F32R)
        gate_bias = sb(lstm_mem, "gate_bias", [P, 4 * MAX_SKIP])

        gcn_mem = ExitStack()
        adj_nat = sb(gcn_mem, "adj_nat", [P, P])
        adjT = sb(gcn_mem, "adjT", [P, P])
        wg0 = sb(gcn_mem, "wg0", [P, DIM])
        wg1 = sb(gcn_mem, "wg1", [P, DIM])
        bg0_rows = sb(gcn_mem, "bg0_rows", [P, DIM])
        bg1_rows = sb(gcn_mem, "bg1_rows", [P, DIM])
        bias0 = sb(gcn_mem, "bias0", [P, 1, DIM])
        bias1 = sb(gcn_mem, "bias1", [P, 1, P])
        wih_raw = sb(gcn_mem, "wih_raw", [P, MAX_SKIP, 4, P])
        whh_raw = sb(gcn_mem, "whh_raw", [P, MAX_SKIP, 4, P])
        b_raw = sb(gcn_mem, "b_raw", [4 * MAX_SKIP, 2, P])
        b_sum = sb(gcn_mem, "b_sum", [4 * MAX_SKIP, P])
        ax = [sb(gcn_mem, f"ax{q}", [P, GB * STEPS]) for q in range(2)]
        pre0 = [sb(gcn_mem, f"pre0{q}", [P, GB, DIM]) for q in range(2)]
        h0 = [sb(gcn_mem, f"h0{q}", [P, GB, DIM]) for q in range(2)]
        ah = [sb(gcn_mem, f"ah{q}", [P, GB * STEPS]) for q in range(2)]
        pre1 = [sb(gcn_mem, f"pre1{q}", [P, GB, STEPS]) for q in range(2)]
        gcn_mem.close()

        step_mem = ExitStack()
        N = 512
        gate = [[sb(step_mem, f"gate{q}{k}", [P, N]) for k in QUARTERS] for q in range(2)]
        in_cell = [sb(step_mem, f"in_cell{q}", [P, N]) for q in range(2)]
        cell = [sb(step_mem, f"cell{q}", [P, N]) for q in range(2)]
        cell_tanh = [sb(step_mem, f"cell_tanh{q}", [P, N]) for q in range(2)]
        hid = [sb(step_mem, f"hid{q}", [P, N]) for q in range(2)]
        hid_hi = [sb(step_mem, f"hid_hi{q}", [P, N], F32R) for q in range(2)]
        hid_lo = [sb(step_mem, f"hid_lo{q}", [P, N], F32R) for q in range(2)]
        step_mem.close()
        lstm_mem.close()

        attn_mem = ExitStack()
        ctx.enter_context(attn_mem)
        hg = [sb(attn_mem, f"hg{q}", [P, GB, STEPS]) for q in range(2)]
        y = [sb(attn_mem, f"y{q}", [P, GB, DIM]) for q in range(2)]
        x1 = [sb(attn_mem, f"x1{q}", [P, GB, DIM]) for q in range(2)]
        x1_all = sb(attn_mem, "x1_all", [P, BATCH, DIM])
        x1T = [sb(attn_mem, f"x1T{q}", [P, GB * STEPS]) for q in range(2)]
        qT = [sb(attn_mem, f"qT{q}", [P, GB * STEPS]) for q in range(2)]
        kT = [sb(attn_mem, f"kT{q}", [P, GB, STEPS]) for q in range(2)]
        k_diag = [sb(attn_mem, f"k_diag{q}", [P, GB, HEADS, STEPS]) for q in range(2)]
        v = [sb(attn_mem, f"v{q}", [P, GB, DIM]) for q in range(2)]
        probs = [sb(attn_mem, f"probs{q}", [P, HEADS, STEPS]) for q in range(2)]
        probsT = [sb(attn_mem, f"probsT{q}", [P, HEADS, STEPS]) for q in range(2)]
        oT = [sb(attn_mem, f"oT{q}", [P, GB * STEPS]) for q in range(2)]
        z = [sb(attn_mem, f"z{q}", [P, GB, DIM]) for q in range(2)]
        res = [sb(attn_mem, f"res{q}", [P, GB, DIM]) for q in range(2)]
        neg_max = [sb(attn_mem, f"neg_max{q}", [P, HEADS]) for q in range(2)]
        den = [sb(attn_mem, f"den{q}", [P, GB * HEADS]) for q in range(2)]
        rden = [sb(attn_mem, f"rden{q}", [P, GB * HEADS, 1]) for q in range(2)]
        stats1 = [sb(attn_mem, f"stats1{q}", [P, GB, 6]) for q in range(2)]
        mv1 = [sb(attn_mem, f"mv1{q}", [P, GB, 2]) for q in range(2)]
        var1 = [sb(attn_mem, f"var1{q}", [P, GB]) for q in range(2)]
        rstd1 = [sb(attn_mem, f"rstd1{q}", [P, GB]) for q in range(2)]
        stats2 = [sb(attn_mem, f"stats2{q}", [P, GB, 6]) for q in range(2)]
        mv2 = [sb(attn_mem, f"mv2{q}", [P, GB, 2]) for q in range(2)]
        var2 = [sb(attn_mem, f"var2{q}", [P, GB]) for q in range(2)]
        rstd2 = [sb(attn_mem, f"rstd2{q}", [P, GB]) for q in range(2)]

        minus_half = sb(attn_mem, "minus_half", [P, GB])
        eps = sb(attn_mem, "eps", [P, GB])

        half_made, var1_done, var2_done = sem("half_made"), sem("var1_done"), sem("var2_done")
        adj_in, gcn_weights_in, lstm_weights_in = sem("adj_in"), sem("gcn_weights_in"), sem("lstm_weights_in")
        qkv_weights_in = sem("qkv_weights_in")
        x_in = [sem(f"x_in{q}") for q in range(2)]
        zeroed, ident_made, ident_bf_made = sem("zeroed"), sem("ident_made"), sem("ident_bf_made")
        prep_pe, prep_act, prep_dve = sem("prep_pe"), sem("prep_act"), sem("prep_dve")
        mask_made = sem("mask_made")
        ax_mm, ax_copied, xw_mm, pre0_done, h0_done = (sem(s) for s in ("ax_mm", "ax_copied", "xw_mm", "pre0_done", "h0_done"))
        ah_mm, ah_copied, hw_mm, pre1_done, hi1_done, lo1_done = (
            sem(s) for s in ("ah_mm", "ah_copied", "hw_mm", "pre1_done", "hi1_done", "lo1_done"))
        wT_mm, w_hi_done, w_lo_done = sem("wT_mm"), sem("w_hi_done"), sem("w_lo_done")
        bias_sum, bias_mm, bias_done = sem("bias_sum"), sem("bias_mm"), sem("bias_done")
        gate_mm, gate_done = sem("gate_mm"), sem("gate_done")
        in_cell_done, kept_done = sem("in_cell_done"), sem("kept_done")
        cell_done, tanh_done, hid_done, hid_hi_done, job_done = (
            sem(s) for s in ("cell_done", "tanh_done", "hid_done", "hid_hi_done", "job_done"))
        hg_done, hgT_mm, y_done, bn1_done, mv1_done, rstd1_done, x1_done, x1_kept = (
            sem(s) for s in ("hg_done", "hgT_mm", "y_done", "bn1_done", "mv1_done", "rstd1_done", "x1_done", "x1_kept"))
        x1T_mm, x1T_done, q_mm, qT_done, k_mm, kT_done, v_mm, v_done = (
            sem(s) for s in ("x1T_mm", "x1T_done", "q_mm", "qT_done", "k_mm", "kT_done", "v_mm", "v_done"))
        k_zeroed = sem("k_zeroed")
        k_in = [sem(f"k_in{q}") for q in range(2)]
        oT_done, o_mm, rden_done, scaled_done, z_done, bn2_done, mv2_done, rstd2_done, res_done = (
            sem(s) for s in ("oT_done", "o_mm", "rden_done", "scaled_done", "z_done", "bn2_done", "mv2_done", "rstd2_done", "res_done"))
        stored = [sem(f"stored{q}") for q in range(2)]
        s_mm, max_done, exp_done, pT_mm, pT_done, pv_mm = (
            sem(s) for s in ("s_mm", "max_done", "exp_done", "pT_mm", "pT_done", "pv_mm"))

        QUADS = 2 * MAX_SKIP - 1
        quads = [(wih_raw, wih_hi, wih_lo, p) for p in range(MAX_SKIP)] + \
                [(whh_raw, whh_hi, whh_lo, p) for p in range(1, MAX_SKIP)]

        def columns(buffer, p):
            return buffer[:, 0:CHUNK[p] * BATCH].rearrange("k (w b) -> k w b", b=BATCH)

        def window(buffer, p, pair, step, side):
            part = buffer[:, 0:WINDOWS[p] * p, :].rearrange("k (w s) b -> k w s b", s=p)
            return part[:, bass.ds(pair * (2 * CHUNK[p]) + side * CHUNK[p], CHUNK[p]), step, :]

        HG_BANK, Q_BANK, K_BANK, O_BANK = 0, 1, 2, 3
        S_BANK, PT_BANK = (4, 5), (6, 7)

        def lstm_schedule(engine, before, job):
            first = [(0, 0), (0, 1)]
            for p in range(1, MAX_SKIP + 1):
                before(p)
                start = 0
                if p == 1:
                    for step, side in first:
                        job(p, 0, step, side, True)
                    start = 1
                with engine.Fori(start, PAIRS[p]) as pair:
                    for step in range(p):
                        for side in range(2):
                            job(p, pair, step, side, False)

        def attention_schedule(engine, body):
            for g in range(-2, 2):
                body(g, g % 2)
            with engine.Fori(0, (GROUPS - 4) // 2) as i:
                for side in range(2):
                    body(i * 2 + (2 + side), side)
            for g in range(GROUPS - 2, GROUPS + 2):
                body(g, g % 2)

        def exists(g):
            return not isinstance(g, int) or 0 <= g < GROUPS

        block = ctx.enter_context(nc.Block())

        @block.sync
        def _(sp):
            sp.dma_start(adj_nat[:], adj).then_inc(adj_in, 16)

            def load_x(g, q):
                reach(sp, ax_mm, g - 1)
                sp.dma_start(xr[q][:], x_groups[g]).then_inc(x_in[q], 16)

            load_x(0, 0)
            sp.dma_start(wg0[:], Wg0).then_inc(gcn_weights_in, 16)
            sp.dma_start(bg0_rows[:], bg0.partition_broadcast(P)).then_inc(gcn_weights_in, 16)
            sp.dma_start(bg1_rows[:], bg1.partition_broadcast(P)).then_inc(gcn_weights_in, 16)
            sp.dma_start(wg1[:], Wg1).then_inc(gcn_weights_in, 16)
            load_x(1, 1)
            with sp.Fori(0, GROUPS // 2 - 1) as i:
                for q in range(2):
                    load_x(i * 2 + (2 + q), q)

            def piece_loads(g, q):
                if exists(g + 2):
                    if isinstance(g, int) and g < 0:
                        sp.wait_ge(ax_mm, GROUPS)
                    reach(sp, y_done, g + 1)
                    sp.dma_start(xr[q][:], x_groups[g + 2]).then_inc(x_in[q], 16)

            def piece_keys(g, q):
                if exists(g + 1):
                    r = (q + 1) % 2
                    if isinstance(g, int) and g < 1:
                        sp.wait_ge(k_zeroed, r + 1)
                    sp.wait_ge(kT_done, g + 2)
                    reach(sp, s_mm, (g - 1) * GB + GB)
                    for h in range(HEADS):
                        rows = slice(h * HEAD_DIM, (h + 1) * HEAD_DIM)
                        sp.dma_start(k_diag[r][rows, :, h, :], kT[r][rows, :, :]).then_inc(k_in[r], 16)

            def piece_store(g, q):
                if exists(g - 2):
                    sp.wait_ge(res_done, g - 1)
                    sp.dma_start(out_groups[g - 2], res[q][:]).then_inc(stored[q], 16)

            def body(g, q):
                piece_loads(g, q)
                piece_keys(g, q)
                piece_store(g, q)

            attention_schedule(sp, body)
            for q in range(2):
                sp.wait_ge(stored[q], 16 * GROUPS // 2)

        @block.gpsimd
        def _(pool):
            pool.memset(ident[:], 0.0).then_inc(zeroed, 1)
            pool.wait_ge(zeroed, 1)
            pool.affine_select(out=ident[:], in_=ident[:], compare_op=ALU.not_equal, fill=1.0, base=0,
                               pattern=[[-1, P]], channel_multiplier=1).then_inc(ident_made, 1)

            pool.wait_ge(job_done, ALL_JOBS)
            pool.memset(minus_half[:], -0.5).then_inc(half_made, 1)
            pool.memset(eps[:], EPS).then_inc(half_made, 1)
            pool.wait_ge(half_made, 2)
            for q in range(2):
                pool.memset(k_diag[q][:], 0.0).then_inc(k_zeroed, 1)

            def body(g, q):
                if exists(g + 2):
                    reach(pool, hgT_mm, g + 1)
                    b0 = (g + 2) * GB
                    pool.tensor_copy(hg[q][:], state[:, :, bass.ds(b0, GB)].rearrange("k t b -> k b t")).then_inc(hg_done, 1)
                if exists(g - 2):
                    pool.wait_ge(mv2_done, g - 1)
                    pool.tensor_tensor(var2[q][:], mv2[q][:, :, 1], eps[:], ALU.add).then_inc(var2_done, 1)
                    pool.wait_ge(var2_done, g - 1)
                    pool.tensor_tensor(rstd2[q][:], var2[q][:], minus_half[:], ALU.pow).then_inc(rstd2_done, 1)
                if exists(g + 2):
                    pool.wait_ge(mv1_done, g + 3)
                    reach(pool, x1_done, (g + 1) * GB)
                    pool.tensor_tensor(var1[q][:], mv1[q][:, :, 1], eps[:], ALU.add).then_inc(var1_done, 1)
                    pool.wait_ge(var1_done, g + 3)
                    pool.tensor_tensor(rstd1[q][:], var1[q][:], minus_half[:], ALU.pow).then_inc(rstd1_done, 1)
                    pool.wait_ge(x1_done, (g + 3) * GB)
                    pool.tensor_copy(x1_all[:, bass.ds(b0, GB), :], x1[q][:]).then_inc(x1_kept, 1)

            attention_schedule(pool, body)

        @block.tensor
        def _(pe):
            pe.wait_ge(ident_made, 1)
            pe.wait_ge(adj_in, 16)
            pe.transpose(bank[:, 0, 0:P], adj_nat[:], ident[:]).then_inc(prep_pe, 1)
            pe.wait_ge(prep_act, 1)
            pe.wait_ge(gcn_weights_in, 64)
            pe.matmul(bank[:, 1, 0:P], adjT[:], bg0_rows[:], start=True, stop=True).then_inc(prep_pe, 1)
            pe.matmul(bank[:, 3, 0:P], bg1_rows[:], adjT[:], start=True, stop=True).then_inc(prep_pe, 1)
            pe.wait_ge(prep_dve, 2)

            def first(g, q):
                pe.wait_ge(x_in[q], g * 8 + (16 - 8 * q))
                reach(pe, ax_copied, g - 1)
                for b in range(GB):
                    mm = pe.matmul(bank[:, q, b * P:(b + 1) * P], xr[q][:, b, :], adjT[:], start=True, stop=True)
                mm.then_inc(ax_mm, 1)

            def second_adj(g, q):
                pe.wait_ge(h0_done, g + 1)
                reach(pe, ah_copied, g - 1)
                for b in range(GB):
                    mm = pe.matmul(bank[:, 4 + q, b * P:(b + 1) * P], h0[q][:, b, :], adjT[:], start=True, stop=True)
                mm.then_inc(ah_mm, 1)

            def first_w(g, q):
                pe.wait_ge(ax_copied, g + 1)
                reach(pe, pre0_done, g - 1)
                for b in range(GB):
                    mm = pe.matmul(bank[:, 2 + q, b * P:(b + 1) * P], ax[q][:, b * P:(b + 1) * P], wg0[:], start=True, stop=True)
                mm.then_inc(xw_mm, 1)

            def second_w(g, q):
                pe.wait_ge(ah_copied, g + 1)
                reach(pe, pre1_done, g - 1)
                pe.matmul(bank[:, 6 + q, :], wg1[:], ah[q][:], start=True, stop=True).then_inc(hw_mm, 1)

            first(0, 0)
            first_w(0, 0)

            def later_first(g, q):
                first(g, q)

            def later_second(g, q):
                second_adj(g, q)
                first_w(g + 1, (q + 1) % 2)
                second_w(g, q)

            for g in (1, 2):
                later_first(g, g % 2)
                later_second(g - 1, (g - 1) % 2)
            with pe.Fori(0, (GROUPS - 4) // 2) as i:
                for side in range(2):
                    later_first(i * 2 + (3 + side), (3 + side) % 2)
                    later_second(i * 2 + (2 + side), side)
            later_first(GROUPS - 1, (GROUPS - 1) % 2)
            later_second(GROUPS - 2, (GROUPS - 2) % 2)
            second_adj(GROUPS - 1, (GROUPS - 1) % 2)
            second_w(GROUPS - 1, (GROUPS - 1) % 2)

            pe.wait_ge(lstm_weights_in, 16 * 4)
            pe.wait_ge(ax_copied, GROUPS)
            for n, (raw, _, _, p) in enumerate(quads):
                reach(pe, w_lo_done, n - 1)
                for k in QUARTERS:
                    mm = pe.transpose(bank[:, n % 2, k * P:(k + 1) * P], raw[:, p, k, :], ident[:])
                mm.then_inc(wT_mm, 1)
            pe.wait_ge(bias_sum, 1)
            pe.wait_ge(pre0_done, GROUPS)
            pe.transpose(bank[:, 2, 0:4 * MAX_SKIP], b_sum[:], ident[0:4 * MAX_SKIP, 0:4 * MAX_SKIP]).then_inc(bias_mm, 1)

            def before(p):
                if p == 1:
                    pe.wait_ge(w_lo_done, QUADS)
                    pe.wait_ge(w_hi_done, QUADS)
                    pe.wait_ge(bias_done, 1)
                    pe.wait_ge(lo1_done, GROUPS)
                    pe.wait_ge(hi1_done, GROUPS)
                else:
                    pe.wait_ge(job_done, JOBS[p].jobs0 - 2)
                    pe.wait_ge(gate_done, JOBS[p].gates0 - gates_before_last(p - 1, 0, 0))

            def product(out_bank, p, k, hi, lo, x_hi, x_lo, first, last):
                pe.matmul(out_bank, lo[:, p - 1, k, :], x_hi, start=first, stop=False)
                pe.matmul(out_bank, hi[:, p - 1, k, :], x_lo, start=False, stop=False)
                return pe.matmul(out_bank, hi[:, p - 1, k, :], x_hi, start=False, stop=last)

            def job(p, pair, step, side, early):
                if not early:
                    pe.wait_ge(gate_done, JOBS[p].gates(pair, step, side) - gates_before_last(p, step, side))
                x_hi, x_lo = (window(s, p, pair, step, side) for s in (state_hi, state_lo))
                gates = gates_of(step)
                outs = {k: columns(bank[:, side * 4 + k, :], p) for k in gates}
                for k in gates:
                    mm = product(outs[k], p, k, wih_hi, wih_lo, x_hi, x_lo, True, step == 0)
                    if step == 0:
                        mm.then_inc(gate_mm, 1)
                if step > 0:
                    pe.wait_ge(job_done, JOBS[p].job(pair, step, side) - 1)
                    for k in gates:
                        product(outs[k], p, k, whh_hi, whh_lo, columns(hid_hi[side], p), columns(hid_lo[side], p),
                                False, True).then_inc(gate_mm, 1)

            lstm_schedule(pe, before, job)

            def piece_hgT(g, q):
                if not exists(g):
                    return
                pe.wait_ge(hg_done, g + 1)
                reach(pe, x1T_done, g)
                for b in range(GB):
                    mm = pe.transpose(bank[:, HG_BANK, b * P:(b + 1) * P], hg[q][:, b, :], ident[:])
                mm.then_inc(hgT_mm, 1)

            def piece_x1T(g, q):
                if not exists(g):
                    return
                pe.wait_ge(x1_done, (g + 1) * GB)
                for b in range(GB):
                    mm = pe.transpose(bank[:, HG_BANK, b * P:(b + 1) * P], x1[q][:, b, :], ident[:])
                mm.then_inc(x1T_mm, 1)

            def piece_qk(g, q):
                if not exists(g):
                    return
                if isinstance(g, int) and g == 0:
                    pe.wait_ge(qkv_weights_in, 16)
                pe.wait_ge(x1T_done, g + 1)
                reach(pe, v_done, g)
                pe.matmul(bank[:, Q_BANK, :], wqkv[:, 0:DIM], x1T[q][:], start=True, stop=True).then_inc(q_mm, 1)
                reach(pe, scaled_done, g - 2)
                pe.matmul(bank[:, K_BANK, :], wqkv[:, DIM:2 * DIM], x1T[q][:], start=True, stop=True).then_inc(k_mm, 1)

            def piece_v(g, q):
                if not exists(g):
                    return
                pe.wait_ge(qT_done, g + 1)
                for b in range(GB):
                    mm = pe.matmul(bank[:, Q_BANK, b * P:(b + 1) * P], x1T[q][:, b * P:(b + 1) * P],
                                   wqkv[:, 2 * DIM:3 * DIM], start=True, stop=True)
                mm.then_inc(v_mm, 1)

            def piece_o(g, q):
                if not exists(g):
                    return
                pe.wait_ge(oT_done, g + 1)
                reach(pe, kT_done, g + 2 if not isinstance(g, int) else min(g + 2, GROUPS))
                for b in range(GB):
                    mm = pe.transpose(bank[:, K_BANK, b * P:(b + 1) * P], oT[q][:, b * P:(b + 1) * P], ident[:])
                mm.then_inc(o_mm, 1)

            def scores(g, q, b):
                if not exists(g):
                    return
                n = g * GB + b
                if b == 0:
                    pe.wait_ge(k_in[q], g * 32 + (64 - 32 * q))
                reach(pe, exp_done, n - 1)
                if isinstance(g, int) and g == 0 and b == 0:
                    pe.wait_ge(mask_made, 1)
                    pe.wait_ge(ident_bf_made, 1)
                out_bank = bank[:, S_BANK[b % 2], :].rearrange("i (h j) -> i h j", h=HEADS)
                pe.matmul(out_bank, qT[q][:, b * P:(b + 1) * P], k_diag[q][:, b, :, :], start=True, stop=False)
                pe.matmul(out_bank, ident_bf[:], mask[:].to_broadcast([P, HEADS, P]), start=False, stop=True).then_inc(s_mm, 1)

            def turn_probs(g, b):
                if not exists(g):
                    return
                n = g * GB + b
                pe.wait_ge(exp_done, n + 1)
                reach(pe, pT_done, n - 1)
                for h in range(HEADS):
                    mm = pe.transpose(bank[:, PT_BANK[b % 2], h * P:(h + 1) * P], probs[b % 2][:, h, :], ident[:])
                mm.then_inc(pT_mm, 1)

            def values(g, q, b):
                if not exists(g):
                    return
                n = g * GB + b
                pe.wait_ge(pT_done, n + 1)
                if b == 0:
                    pe.wait_ge(v_done, g + 1)
                    reach(pe, oT_done, g)
                for h in range(HEADS):
                    rows = slice(h * HEAD_DIM, (h + 1) * HEAD_DIM)
                    mm = pe.matmul(bank[rows, O_BANK, b * P:(b + 1) * P], v[q][:, b, rows], probsT[b % 2][:, h, :],
                                   start=True, stop=True)
                mm.then_inc(pv_mm, 1)

            def body(g, q):
                r = (q + 1) % 2
                scores(g, q, 0)
                piece_x1T(g + 1, r)
                turn_probs(g - 1, 3)
                values(g - 1, r, 2)
                scores(g, q, 1)
                piece_hgT(g + 2, q)
                piece_qk(g + 1, r)
                turn_probs(g, 0)
                values(g - 1, r, 3)
                scores(g, q, 2)
                piece_v(g + 1, r)
                turn_probs(g, 1)
                values(g, q, 0)
                scores(g, q, 3)
                piece_o(g - 1, r)
                turn_probs(g, 2)
                values(g, q, 1)

            attention_schedule(pe, body)

        @block.scalar
        def _(act):
            act.dma_start(wih_raw[:], Wih.rearrange("p (q r) k -> r p q k", r=P)).then_inc(lstm_weights_in, 16)
            act.dma_start(whh_raw[:], Whh.rearrange("p (q r) k -> r p q k", r=P)).then_inc(lstm_weights_in, 16)
            act.dma_start(b_raw[:, 0, :], bih.rearrange("p (q r) -> (p q) r", r=P)).then_inc(lstm_weights_in, 16)
            act.dma_start(b_raw[:, 1, :], bhh.rearrange("p (q r) -> (p q) r", r=P)).then_inc(lstm_weights_in, 16)
            act.dma_start(wqkv[:], Wqkv).then_inc(qkv_weights_in, 16)
            act.wait_ge(prep_pe, 1)
            act.copy(adjT[:], bank[:, 0, 0:P]).then_inc(prep_act, 1)
            act.wait_ge(ident_made, 1)
            act.copy(ident_bf[:], ident[:]).then_inc(ident_bf_made, 1)

            def first(g, q):
                act.wait_ge(ax_mm, g + 1)
                reach(act, xw_mm, g - 1)
                act.copy(ax[q][:], bank[:, q, :]).then_inc(ax_copied, 1)

            def relu0(g, q):
                act.wait_ge(pre0_done, g + 1)
                reach(act, ah_mm, g - 1)
                act.activation(h0[q][:], pre0[q][:], ACT.Relu).then_inc(h0_done, 1)

            def second_copy(g, q):
                act.wait_ge(ah_mm, g + 1)
                reach(act, hw_mm, g - 1)
                act.copy(ah[q][:], bank[:, 4 + q, :]).then_inc(ah_copied, 1)

            def relu1(g, q):
                act.wait_ge(pre1_done, g + 1)
                act.activation(state_hi[:, :, bass.ds(g * GB, GB)].rearrange("k t b -> k b t"), pre1[q][:],
                               ACT.Relu).then_inc(hi1_done, 1)

            first(0, 0)
            relu0(0, 0)

            def second(g, q):
                second_copy(g, q)
                relu0(g + 1, (q + 1) % 2)
                relu1(g, q)

            for g in (1, 2):
                first(g, g % 2)
                second(g - 1, (g - 1) % 2)
            with act.Fori(0, (GROUPS - 4) // 2) as i:
                for side in range(2):
                    first(i * 2 + (3 + side), (3 + side) % 2)
                    second(i * 2 + (2 + side), side)
            first(GROUPS - 1, (GROUPS - 1) % 2)
            second(GROUPS - 2, (GROUPS - 2) % 2)
            second_copy(GROUPS - 1, (GROUPS - 1) % 2)
            relu1(GROUPS - 1, (GROUPS - 1) % 2)

            for n, (_, hi, _, p) in enumerate(quads):
                act.wait_ge(wT_mm, n + 1)
                act.copy(hi[:, p, :, :], bank[:, n % 2, :].rearrange("k (q r) -> k q r", q=4)).then_inc(w_hi_done, 1)
            act.wait_ge(bias_mm, 1)
            act.copy(gate_bias[:], bank[:, 2, 0:4 * MAX_SKIP]).then_inc(bias_done, 1)
            act.wait_ge(bias_done, 1)

            def job(p, pair, step, side, early):
                if not early:
                    act.wait_ge(job_done, JOBS[p].job(pair, step, side) - 1)
                before = JOBS[p].gates(pair, step, side)
                for n, k in enumerate(gates_of(step)):
                    act.wait_ge(gate_mm, before + (n + 1))
                    act.activation(columns(gate[side][k], p), columns(bank[:, side * 4 + k, :], p), GATE_FUNCTION[k],
                                   bias=gate_bias[:, 4 * (p - 1) + k:4 * (p - 1) + k + 1]).then_inc(gate_done, 1)
                act.wait_ge(cell_done, JOBS[p].job(pair, step, side) + 1)
                act.activation(columns(cell_tanh[side], p), columns(cell[side], p), ACT.Tanh).then_inc(tanh_done, 1)

            lstm_schedule(act, lambda p: None, job)

            def copy_x1T(g, q):
                if not exists(g):
                    return
                act.wait_ge(x1T_mm, g + 1)
                reach(act, v_mm, g - 1)
                act.copy(x1T[q][:], bank[:, HG_BANK, :]).then_inc(x1T_done, 1)

            def copy_qT(g, q):
                if not exists(g):
                    return
                act.wait_ge(q_mm, g + 1)
                reach(act, s_mm, (g - 1) * GB)
                act.mul(qT[q][:], bank[:, Q_BANK, :], HEAD_DIM ** -0.5).then_inc(qT_done, 1)

            def exponentials(g, q, b):
                if not exists(g):
                    return
                n = g * GB + b
                act.wait_ge(max_done, n + 1)
                reach(act, pT_mm, n - 1)
                if b == 0:
                    reach(act, rden_done, g - 1)
                for h in range(HEADS):
                    e = act.activation(probs[b % 2][:, h, :], bank[:, S_BANK[b % 2], h * P:(h + 1) * P], ACT.Exp,
                                       bias=neg_max[b % 2][:, h:h + 1], accum_out=den[q][:, b * HEADS + h:b * HEADS + h + 1])
                e.then_inc(exp_done, 1)

            def copy_pT(g, b):
                if not exists(g):
                    return
                n = g * GB + b
                act.wait_ge(pT_mm, n + 1)
                reach(act, pv_mm, n - 1)
                act.copy(probsT[b % 2][:], bank[:, PT_BANK[b % 2], :].rearrange("j (h i) -> j h i", h=HEADS)).then_inc(pT_done, 1)

            def body(g, q):
                r = (q + 1) % 2
                exponentials(g, q, 0)
                copy_x1T(g + 1, r)
                copy_pT(g - 1, 3)
                exponentials(g, q, 1)
                copy_qT(g + 1, r)
                copy_pT(g, 0)
                exponentials(g, q, 2)
                copy_pT(g, 1)
                exponentials(g, q, 3)
                copy_pT(g, 2)

            attention_schedule(act, body)

        @block.vector
        def _(dve):
            dve.wait_ge(adj_in, 16)
            dve.tensor_scalar(mask[:, 0, :], adj_nat[:], 0.0, MASKED, ALU.is_equal, ALU.mult).then_inc(mask_made, 1)
            dve.wait_ge(prep_pe, 3)
            dve.tensor_copy(bias0[:, 0, :], bank[:, 1, 0:P]).then_inc(prep_dve, 1)
            dve.tensor_copy(bias1[:, 0, :], bank[:, 3, 0:P]).then_inc(prep_dve, 1)
            dve.wait_ge(prep_dve, 2)
            dve.wait_ge(lstm_weights_in, 16 * 4)
            dve.tensor_tensor(b_sum[:], b_raw[:, 0, :], b_raw[:, 1, :], ALU.add).then_inc(bias_sum, 1)

            def add0(g, q):
                dve.wait_ge(xw_mm, g + 1)
                reach(dve, h0_done, g - 1)
                dve.tensor_tensor(pre0[q][:], bank[:, 2 + q, :].rearrange("t (b d) -> t b d", b=GB),
                                  bias0[:].to_broadcast([P, GB, DIM]), ALU.add).then_inc(pre0_done, 1)

            def add1(g, q):
                dve.wait_ge(hw_mm, g + 1)
                reach(dve, lo1_done, g - 1)
                dve.tensor_tensor(pre1[q][:], bank[:, 6 + q, :].rearrange("k (b t) -> k b t", b=GB),
                                  bias1[:].to_broadcast([P, GB, STEPS]), ALU.add).then_inc(pre1_done, 1)

            def low1(g, q):
                dve.wait_ge(hi1_done, g + 1)
                columns_of_group = bass.ds(g * GB, GB)
                dve.scalar_tensor_tensor(out=state_lo[:, :, columns_of_group].rearrange("k t b -> k b t"), in0=pre1[q][:],
                                         scalar=0.0,
                                         in1=state_hi[:, :, columns_of_group].rearrange("k t b -> k b t").bitcast(F32),
                                         op0=ALU.max, op1=ALU.subtract).then_inc(lo1_done, 1)

            add0(0, 0)

            def second(g, q):
                add0(g + 1, (q + 1) % 2)
                add1(g, q)
                low1(g, q)

            for g in (1, 2):
                second(g - 1, (g - 1) % 2)
            with dve.Fori(0, (GROUPS - 4) // 2) as i:
                for side in range(2):
                    second(i * 2 + (2 + side), side)
            second(GROUPS - 2, (GROUPS - 2) % 2)
            add1(GROUPS - 1, (GROUPS - 1) % 2)
            low1(GROUPS - 1, (GROUPS - 1) % 2)

            for n, (_, hi, lo, p) in enumerate(quads):
                dve.wait_ge(w_hi_done, n + 1)
                dve.tensor_tensor(lo[:, p, :, :], bank[:, n % 2, :].rearrange("k (q r) -> k q r", q=4),
                                  hi[:, p, :, :].bitcast(F32), ALU.subtract).then_inc(w_lo_done, 1)

            def job(p, pair, step, side, early):
                j = JOBS[p].job(pair, step, side)
                g0 = JOBS[p].gates(pair, step, side)
                i_, f_, g_, o_ = (columns(gate[side][k], p) for k in QUARTERS)
                c = columns(cell[side], p)
                dve.wait_ge(gate_done, g0 + 2)
                if step == 0:
                    dve.tensor_tensor(c, i_, g_, ALU.mult).then_inc(cell_done, 1)
                else:
                    m = JOBS[p].later(pair, step, side)
                    new = columns(in_cell[side], p)
                    dve.tensor_tensor(new, i_, g_, ALU.mult).then_inc(in_cell_done, 1)
                    dve.wait_ge(gate_done, g0 + 3)
                    dve.tensor_tensor(c, f_, c, ALU.mult).then_inc(kept_done, 1)
                    dve.wait_ge(in_cell_done, m + 1)
                    dve.wait_ge(kept_done, m + 1)
                    dve.tensor_tensor(c, c, new, ALU.add).then_inc(cell_done, 1)
                if step == p - 1:
                    full, hi, lo = (window(s, p, pair, step, side) for s in (state, state_hi, state_lo))
                else:
                    full, hi, lo = (columns(s[side], p) for s in (hid, hid_hi, hid_lo))
                dve.wait_ge(tanh_done, j + 1)
                dve.tensor_tensor(full, o_, columns(cell_tanh[side], p), ALU.mult).then_inc(hid_done, 1)
                dve.wait_ge(hid_done, j + 1)
                dve.tensor_copy(hi, full).then_inc(hid_hi_done, 1)
                dve.wait_ge(hid_hi_done, j + 1)
                dve.tensor_tensor(lo, full, hi.bitcast(F32), ALU.subtract).then_inc(job_done, 1)

            lstm_schedule(dve, lambda p: None, job)

            def maximum(g, b):
                if not exists(g):
                    return
                n = g * GB + b
                dve.wait_ge(s_mm, n + 1)
                reach(dve, exp_done, n - 1)
                dve.tensor_reduce(neg_max[b % 2][:], bank[:, S_BANK[b % 2], :].rearrange("i (h j) -> i h j", h=HEADS),
                                  AX_X, ALU.max, negate=True).then_inc(max_done, 1)

            def partial_stats(source, stats, bn_done):
                for b in range(GB):
                    last = dve.bn_stats(stats[:, b, :], source[:, b, :])
                last.then_inc(bn_done, 1)

            def mean_var(g, stats, mv, mv_done):
                if not exists(g):
                    return
                for b in range(GB):
                    last = dve.bn_aggr(mv[:, b, :], stats[:, b, :])
                last.then_inc(mv_done, 1)

            def stats_ready(g, bn_done):
                if exists(g):
                    dve.wait_ge(bn_done, g + 1)

            def residual1(g, q):
                if not exists(g):
                    return
                dve.wait_ge(hgT_mm, g + 1)
                dve.wait_ge(x_in[q], g * 8 + (16 - 8 * q) + 16 * (GROUPS // 2))
                reach(dve, x1_done, (g - 1) * GB)
                dve.tensor_tensor(y[q][:], bank[:, HG_BANK, :].rearrange("t (b d) -> t b d", b=GB), xr[q][:],
                                  ALU.add).then_inc(y_done, 1)
                dve.wait_ge(y_done, g + 1)
                partial_stats(y[q], stats1[q], bn1_done)

            def norm1(g, q):
                if not exists(g):
                    return
                dve.wait_ge(rstd1_done, g + 1)
                reach(dve, x1_kept, g - 1)
                reach(dve, x1T_mm, g - 1)
                for b in range(GB):
                    dve.tensor_scalar(x1[q][:, b, :], y[q][:, b, :], mv1[q][:, b, 0:1], rstd1[q][:, b:b + 1],
                                      ALU.subtract, ALU.mult).then_inc(x1_done, 1)

            def copy_kT(g, q):
                if not exists(g):
                    return
                dve.wait_ge(k_mm, g + 1)
                reach(dve, k_in[q], (g - 1) * 32 + 32 * (1 - q) if not isinstance(g, int) else 64 * (g // 2))
                dve.tensor_copy(kT[q][:], bank[:, K_BANK, :].rearrange("k (b t) -> k b t", b=GB)).then_inc(kT_done, 1)

            def copy_v(g, q):
                if not exists(g):
                    return
                dve.wait_ge(v_mm, g + 1)
                reach(dve, pv_mm, (g - 1) * GB)
                dve.tensor_copy(v[q][:], bank[:, Q_BANK, :].rearrange("t (b d) -> t b d", b=GB)).then_inc(v_done, 1)

            def copy_oT(g, q):
                if not exists(g):
                    return
                dve.wait_ge(pv_mm, (g + 1) * GB)
                reach(dve, o_mm, g - 1)
                dve.tensor_copy(oT[q][:], bank[:, O_BANK, :]).then_inc(oT_done, 1)

            def reciprocal(g, q):
                if not exists(g):
                    return
                dve.wait_ge(exp_done, (g + 1) * GB)
                reach(dve, scaled_done, g - 1)
                dve.reciprocal(rden[q][:, :, 0], den[q][:]).then_inc(rden_done, 1)

            def residual2(g, q):
                if not exists(g):
                    return
                dve.wait_ge(o_mm, g + 1)
                dve.wait_ge(rden_done, g + 1)
                dve.tensor_tensor(z[q][:].rearrange("t b (h d) -> t (b h) d", h=HEADS),
                                  bank[:, K_BANK, :].rearrange("t (c d) -> t c d", d=HEAD_DIM),
                                  rden[q][:].to_broadcast([P, GB * HEADS, HEAD_DIM]), ALU.mult).then_inc(scaled_done, 1)
                dve.wait_ge(scaled_done, g + 1)
                dve.wait_ge(x1_kept, g + 1)
                dve.tensor_tensor(z[q][:], z[q][:], x1_all[:, bass.ds(g * GB, GB), :], ALU.add).then_inc(z_done, 1)
                dve.wait_ge(z_done, g + 1)
                partial_stats(z[q], stats2[q], bn2_done)

            def norm2(g, q):
                if not exists(g):
                    return
                dve.wait_ge(rstd2_done, g + 1)
                reach(dve, stored[q], (g - 1) * 8 + 8 * (1 - q) if not isinstance(g, int) else 16 * (g // 2))
                for b in range(GB):
                    last = dve.tensor_scalar(res[q][:, b, :], z[q][:, b, :], mv2[q][:, b, 0:1], rstd2[q][:, b:b + 1],
                                             ALU.subtract, ALU.mult)
                last.then_inc(res_done, 1)

            def body(g, q):
                r = (q + 1) % 2
                maximum(g, 0)
                reciprocal(g - 1, r)
                residual2(g - 2, q)
                stats_ready(g - 2, bn2_done)
                maximum(g, 1)
                mean_var(g - 2, stats2[q], mv2[q], mv2_done)
                copy_kT(g + 1, r)
                residual1(g + 2, q)
                stats_ready(g + 2, bn1_done)
                maximum(g, 2)
                mean_var(g + 2, stats1[q], mv1[q], mv1_done)
                norm2(g - 2, q)
                copy_oT(g - 1, r)
                maximum(g, 3)
                copy_v(g + 1, r)
                norm1(g + 2, q)

            attention_schedule(dve, body)


_INPUTS = ("x", "adj", "L0_gnn_Wg0", "L0_gnn_bg0", "L0_gnn_Wg1", "L0_gnn_bg1", "L0_gnn_Wih", "L0_gnn_Whh",
           "L0_gnn_bih", "L0_gnn_bhh", "L1_gnn_W")


def kernel(**inputs):
    import numpy as np
    import concourse.bacc as bacc
    from concourse.bass_utils import run_bass_kernel_spmd

    nc = bacc.Bacc("TRN2", target_bir_lowering=False, num_devices=1)
    arrays, args = {}, []
    for name in _INPUTS:
        a = np.ascontiguousarray(inputs[name])
        arrays[f"in_{name}"] = a
        args.append(nc.dram_tensor(f"in_{name}", a.shape, mybir.dt.from_np(a.dtype), kind="ExternalInput").ap())
    args.append(nc.dram_tensor("out_dram", (BATCH, STEPS, DIM), F32, kind="ExternalOutput").ap())
    build(nc, *args)
    done = run_bass_kernel_spmd(nc, [arrays], core_ids=[0])
    return done.results[0]["out_dram"]
```

```python
from contextlib import ExitStack

import concourse.bass as bass
from concourse import mybir

ALU = mybir.AluOpType
ACT = mybir.ActivationFunctionType
AX_X = mybir.AxisListType.X
F32 = mybir.dt.float32
F32R = mybir.dt.float32r
BF16 = mybir.dt.bfloat16

BATCH, STEPS, DIM = 64, 128, 128
P = 128
GB = 4
GROUPS = BATCH // GB
HEADS = 4
HEAD_DIM = DIM // HEADS
MAX_SKIP = 4
EPS = 1e-5
MASKED = -1e30
QUARTERS = (0, 1, 2, 3)
GATE_I, GATE_F, GATE_G, GATE_O = QUARTERS
GATE_FUNCTION = {GATE_I: ACT.Sigmoid, GATE_F: ACT.Sigmoid, GATE_G: ACT.Tanh, GATE_O: ACT.Sigmoid}

WINDOWS = {p: STEPS // p for p in range(2, MAX_SKIP + 1)}
CHUNK = {2: 8, 3: 7, 4: 8}
PAIRS = {p: WINDOWS[p] // CHUNK[p] // 2 for p in CHUNK}
assert all(PAIRS[p] * 2 * CHUNK[p] == WINDOWS[p] for p in CHUNK)


def gates_of(step):
    return (GATE_I, GATE_G, GATE_O) if step == 0 else (GATE_I, GATE_G, GATE_F, GATE_O)


class Job:

    def __init__(self, p, pair, step, side, number, gates, later, turn, gates_of_last, distance):
        self.p, self.pair, self.step, self.side = p, pair, step, side
        self.number, self.gates, self.later, self.turn = number, gates, later, turn
        self.gates_of_last = gates_of_last
        self.before = number - distance + 1


LAST_PAIR = {p: PAIRS[p] - 1 for p in PAIRS}
START = {2: (2, 6, 0)}
for _p in range(3, MAX_SKIP + 1):
    START[_p] = tuple(n + PAIRS[_p - 1] * m for n, m in
                      zip(START[_p - 1], (2 * (_p - 1), 8 * (_p - 2) + 6, 2 * (_p - 2))))
ALL_JOBS = 2 + sum(2 * p * PAIRS[p] for p in PAIRS) - 2


def first_jobs():
    return [Job(2, 0, 0, side, side, 3 * side, 0, side, 3, 1) for side in range(2)]


def body_jobs(p, pair):
    last = isinstance(pair, int) and pair == LAST_PAIR[p]
    final = last and p == MAX_SKIP
    after = (p + 1, 0) if last else (p, pair + 1)
    order = [(p, pair, step, side) for step in range(1, p - 1) for side in range(2)]
    order.append((p, pair, p - 1, 0))
    if not final:
        order.append((*after, 0, 0))
    order.append((p, pair, p - 1, 1))
    if not final:
        order.append((*after, 0, 1))
    place = {(0, 0): -3, (0, 1): -1}
    if p == 2 and isinstance(pair, int) and pair == 0:
        place = {(0, 0): -2, (0, 1): -1}
    jobs0, gates0, later0 = START[p]
    gates, later, gates_of_last, jobs = 0, 0, 3, []
    for n, (p_, pair_, step, side) in enumerate(order):
        distance = n - place[step - 1, side] if step > 0 else 1
        jobs.append(Job(p_, pair_, step, side, pair * (2 * p) + (jobs0 + n), pair * (8 * (p - 1) + 6) + (gates0 + gates),
                        pair * (2 * (p - 1)) + (later0 + later), n % 2, gates_of_last, distance))
        if step > 0:
            place[step, side] = n
            later += 1
        gates_of_last = len(gates_of(step))
        gates += gates_of_last
    return jobs


def reach(engine, semaphore, count):
    if not isinstance(count, int) or count > 0:
        engine.wait_ge(semaphore, count)


def build(nc, x, adj, Wg0, bg0, Wg1, bg1, Wih, Whh, bih, bhh, Wqkv, out):
    x_groups = x.rearrange("(g b) t d -> g t b d", b=GB)
    out_groups = out.rearrange("(g b) t d -> g t b d", b=GB)

    with ExitStack() as ctx:
        def sem(name):
            return ctx.enter_context(nc.semaphore(name))

        def sb(stack, name, shape, dtype=F32):
            return stack.enter_context(nc.sbuf_tensor(name, shape, dtype))

        bank = ctx.enter_context(nc.psum_tensor("bank", [P, 8, 512], F32))

        ident = sb(ctx, "ident", [P, P])
        ident_bf = sb(ctx, "ident_bf", [P, P], BF16)
        mask = sb(ctx, "mask", [P, 1, P], BF16)
        wqkv = sb(ctx, "wqkv", [P, 3 * DIM])
        xr = [sb(ctx, f"xr{q}", [P, GB, DIM]) for q in range(2)]
        state = sb(ctx, "state", [P, STEPS, BATCH])

        k_diag = [sb(ctx, f"k_diag{q}", [P, GB, HEADS, STEPS]) for q in range(2)]

        lstm_mem = ExitStack()
        state_hi = sb(lstm_mem, "state_hi", [P, STEPS, BATCH], F32R)
        state_lo = sb(lstm_mem, "state_lo", [P, STEPS, BATCH], F32R)
        wih_hi = sb(lstm_mem, "wih_hi", [P, MAX_SKIP, 4, P], F32R)
        wih_lo = sb(lstm_mem, "wih_lo", [P, MAX_SKIP, 4, P], F32R)
        whh_hi = sb(lstm_mem, "whh_hi", [P, MAX_SKIP, 4, P], F32R)
        whh_lo = sb(lstm_mem, "whh_lo", [P, MAX_SKIP, 4, P], F32R)
        gate_bias = sb(lstm_mem, "gate_bias", [P, 4 * MAX_SKIP])

        gcn_mem = ExitStack()
        adj_nat = sb(gcn_mem, "adj_nat", [P, P])
        adjT = sb(gcn_mem, "adjT", [P, P])
        wg0 = sb(gcn_mem, "wg0", [P, DIM])
        wg1 = sb(gcn_mem, "wg1", [P, DIM])
        bg0_rows = sb(gcn_mem, "bg0_rows", [P, DIM])
        bg1_rows = sb(gcn_mem, "bg1_rows", [P, DIM])
        bias0 = sb(gcn_mem, "bias0", [P, 1, DIM])
        bias1 = sb(gcn_mem, "bias1", [P, 1, P])
        raw = state[:].rearrange("k t b -> k (t b)")[:, 0:2 * MAX_SKIP * 4 * P].rearrange(
            "k (w p q r) -> k w p q r", w=2, p=MAX_SKIP, q=4)
        wih_raw, whh_raw = raw[:, 0], raw[:, 1]
        b_raw = sb(gcn_mem, "b_raw", [4 * MAX_SKIP, 2, P])
        b_sum = sb(gcn_mem, "b_sum", [4 * MAX_SKIP, P])
        ax = [sb(gcn_mem, f"ax{q}", [P, GB * STEPS]) for q in range(2)]
        pre0 = [sb(gcn_mem, f"pre0{q}", [P, GB, DIM]) for q in range(2)]
        h0 = [sb(gcn_mem, f"h0{q}", [P, GB, DIM]) for q in range(2)]
        ah = [sb(gcn_mem, f"ah{q}", [P, GB * STEPS]) for q in range(2)]
        pre1 = [sb(gcn_mem, f"pre1{q}", [P, GB * STEPS]) for q in range(2)]
        h1_hi = [sb(gcn_mem, f"h1_hi{q}", [P, GB * STEPS], F32R) for q in range(2)]
        h1_lo = [sb(gcn_mem, f"h1_lo{q}", [P, GB * STEPS], F32R) for q in range(2)]
        gate1 = [[sb(gcn_mem, f"gate1{q}{k}", [P, GB * STEPS]) for k in range(3)] for q in range(2)]
        cell1 = [sb(gcn_mem, f"cell1{q}", [P, GB * STEPS]) for q in range(2)]
        cell1_tanh = [sb(gcn_mem, f"cell1_tanh{q}", [P, GB * STEPS]) for q in range(2)]
        gcn_mem.close()

        step_mem = ExitStack()
        N = 512
        gate = [[sb(step_mem, f"gate{q}{k}", [P, N]) for k in QUARTERS] for q in range(2)]
        in_cell = [sb(step_mem, f"in_cell{q}", [P, N]) for q in range(2)]
        cell = [sb(step_mem, f"cell{q}", [P, N]) for q in range(2)]
        cell_tanh = [sb(step_mem, f"cell_tanh{q}", [P, N]) for q in range(2)]
        hid = [sb(step_mem, f"hid{q}", [P, N]) for q in range(2)]
        hid_hi = [sb(step_mem, f"hid_hi{q}", [P, N], F32R) for q in range(2)]
        hid_lo = [sb(step_mem, f"hid_lo{q}", [P, N], F32R) for q in range(2)]
        step_mem.close()
        lstm_mem.close()

        attn_mem = ExitStack()
        ctx.enter_context(attn_mem)
        hg = [sb(attn_mem, f"hg{q}", [P, GB, STEPS]) for q in range(2)]
        y = [sb(attn_mem, f"y{q}", [P, GB, DIM]) for q in range(2)]
        x1 = [sb(attn_mem, f"x1{q}", [P, GB, DIM]) for q in range(2)]
        x1_all = sb(attn_mem, "x1_all", [P, BATCH, DIM])
        x1T = [sb(attn_mem, f"x1T{q}", [P, GB * STEPS]) for q in range(2)]
        qT = [sb(attn_mem, f"qT{q}", [P, GB * STEPS]) for q in range(2)]
        kT = [sb(attn_mem, f"kT{q}", [P, GB, STEPS]) for q in range(2)]
        v = [sb(attn_mem, f"v{q}", [P, GB, DIM]) for q in range(2)]
        probs = [sb(attn_mem, f"probs{q}", [P, HEADS, STEPS]) for q in range(2)]
        probsT = [sb(attn_mem, f"probsT{q}", [P, HEADS, STEPS]) for q in range(2)]
        oT = [sb(attn_mem, f"oT{q}", [P, GB * STEPS]) for q in range(2)]
        z = [sb(attn_mem, f"z{q}", [P, GB, DIM]) for q in range(2)]
        res = [sb(attn_mem, f"res{q}", [P, GB, DIM]) for q in range(2)]
        neg_max = [sb(attn_mem, f"neg_max{q}", [P, HEADS]) for q in range(2)]
        den = [sb(attn_mem, f"den{q}", [P, GB * HEADS]) for q in range(2)]
        rden = [sb(attn_mem, f"rden{q}", [P, GB * HEADS, 1]) for q in range(2)]
        stats1 = [sb(attn_mem, f"stats1{q}", [P, GB, 6]) for q in range(2)]
        mv1 = [sb(attn_mem, f"mv1{q}", [P, GB, 2]) for q in range(2)]
        var1 = [sb(attn_mem, f"var1{q}", [P, GB]) for q in range(2)]
        rstd1 = [sb(attn_mem, f"rstd1{q}", [P, GB]) for q in range(2)]
        stats2 = [sb(attn_mem, f"stats2{q}", [P, GB, 6]) for q in range(2)]
        mv2 = [sb(attn_mem, f"mv2{q}", [P, GB, 2]) for q in range(2)]
        var2 = [sb(attn_mem, f"var2{q}", [P, GB]) for q in range(2)]
        rstd2 = [sb(attn_mem, f"rstd2{q}", [P, GB]) for q in range(2)]

        minus_half = sb(attn_mem, "minus_half", [P, GB])
        eps = sb(attn_mem, "eps", [P, GB])

        half_made, var1_done, var2_done = sem("half_made"), sem("var1_done"), sem("var2_done")
        adj_in, gcn_weights_in, lstm_weights_in = sem("adj_in"), sem("gcn_weights_in"), sem("lstm_weights_in")
        qkv_weights_in = sem("qkv_weights_in")
        x_in = [sem(f"x_in{q}") for q in range(2)]
        zeroed, ident_made, ident_bf_made = sem("zeroed"), sem("ident_made"), sem("ident_bf_made")
        prep_pe, prep_act, prep_dve = sem("prep_pe"), sem("prep_act"), sem("prep_dve")
        mask_made = sem("mask_made")
        ax_mm, ax_copied, xw_mm, pre0_done, h0_done = (sem(s) for s in ("ax_mm", "ax_copied", "xw_mm", "pre0_done", "h0_done"))
        ah_mm, ah_copied, hw_mm, pre1_done, hi1_done, lo1_done = (
            sem(s) for s in ("ah_mm", "ah_copied", "hw_mm", "pre1_done", "hi1_done", "lo1_done"))
        wT_mm, w_hi_done, w_lo_done = sem("wT_mm"), sem("w_hi_done"), sem("w_lo_done")
        bias_sum, bias_mm, bias_done = sem("bias_sum"), sem("bias_mm"), sem("bias_done")
        gate1_mm, gate1_done, cell1_done, tanh1_done, hid1_done, hid1_hi_done, pass1_done = (
            sem(s) for s in ("gate1_mm", "gate1_done", "cell1_done", "tanh1_done", "hid1_done", "hid1_hi_done", "pass1_done"))
        gate_mm, gate_done = sem("gate_mm"), sem("gate_done")
        in_cell_done, kept_done = sem("in_cell_done"), sem("kept_done")
        cell_done, tanh_done, hid_done, hid_hi_done, job_done = (
            sem(s) for s in ("cell_done", "tanh_done", "hid_done", "hid_hi_done", "job_done"))
        hg_done, hgT_mm, y_done, bn1_done, mv1_done, rstd1_done, x1_done, x1_kept = (
            sem(s) for s in ("hg_done", "hgT_mm", "y_done", "bn1_done", "mv1_done", "rstd1_done", "x1_done", "x1_kept"))
        x1T_mm, x1T_done, q_mm, qT_done, k_mm, kT_done, v_mm, v_done = (
            sem(s) for s in ("x1T_mm", "x1T_done", "q_mm", "qT_done", "k_mm", "kT_done", "v_mm", "v_done"))
        k_zeroed = sem("k_zeroed")
        k_in = [sem(f"k_in{q}") for q in range(2)]
        oT_done, o_mm, rden_done, scaled_done, z_done, bn2_done, mv2_done, rstd2_done, res_done = (
            sem(s) for s in ("oT_done", "o_mm", "rden_done", "scaled_done", "z_done", "bn2_done", "mv2_done", "rstd2_done", "res_done"))
        stored = [sem(f"stored{q}") for q in range(2)]
        s_mm, max_done, exp_done, pT_mm, pT_done, pv_mm = (
            sem(s) for s in ("s_mm", "max_done", "exp_done", "pT_mm", "pT_done", "pv_mm"))

        QUADS = 2 * MAX_SKIP - 1
        quads = [(wih_raw, wih_hi, wih_lo, p) for p in range(MAX_SKIP)] + \
                [(whh_raw, whh_hi, whh_lo, p) for p in range(1, MAX_SKIP)]

        def columns(buffer, p):
            return buffer[:, 0:CHUNK[p] * BATCH].rearrange("k (w b) -> k w b", b=BATCH)

        def window(buffer, j):
            n, p = CHUNK[j.p], j.p
            part = buffer[:, 0:WINDOWS[p] * p, :].rearrange("k (w s) b -> k w s b", s=p)
            return part[:, bass.ds(j.pair * (2 * n) + j.side * n, n), j.step, :]

        HG_BANK, Q_BANK, K_BANK, O_BANK = 0, 1, 2, 3
        S_BANK, PT_BANK = (4, 5), (6, 7)
        AX_BANK, XW_BANK, AH_BANK, HW_BANK, GATE1_BANK, W_BANK = 0, 1, 2, 3, (4, 5, 6), 7

        def graph_schedule(engine, body):
            for g in range(4):
                body(g, g % 2)
            with engine.Fori(0, (GROUPS - 4) // 2) as i:
                for side in range(2):
                    body(i * 2 + (4 + side), side)
            for g in range(GROUPS, GROUPS + 4):
                body(g, g % 2)

        def weight_quads(g):
            if not isinstance(g, int) or g > 2:
                return ()
            return ((0, 1), (2, 3, 4), (5, 6))[g]

        def lstm_schedule(engine, job):
            for j in first_jobs():
                job(j)
            for p in range(2, MAX_SKIP + 1):
                start = 1 if p == 2 else 0
                if start:
                    for j in body_jobs(p, 0):
                        job(j)
                if LAST_PAIR[p] - start > 1:
                    with engine.Fori(start, LAST_PAIR[p]) as pair:
                        for j in body_jobs(p, pair):
                            job(j)
                else:
                    for j in body_jobs(p, start):
                        job(j)
                for j in body_jobs(p, LAST_PAIR[p]):
                    job(j)

        def attention_schedule(engine, body):
            for g in range(-2, 4):
                body(g, g % 2)
            with engine.Fori(0, (GROUPS - 6) // 2) as i:
                for side in range(2):
                    body(i * 2 + (4 + side), side)
            for g in range(GROUPS - 2, GROUPS + 2):
                body(g, g % 2)

        def exists(g):
            return not isinstance(g, int) or 0 <= g < GROUPS

        block = ctx.enter_context(nc.Block())

        @block.sync
        def _(sp):
            sp.dma_start(adj_nat[:], adj).then_inc(adj_in, 16)

            def load_x(g, q):
                reach(sp, ax_mm, g - 1)
                sp.dma_start(xr[q][:], x_groups[g]).then_inc(x_in[q], 16)

            load_x(0, 0)
            sp.dma_start(wg0[:], Wg0).then_inc(gcn_weights_in, 16)
            sp.dma_start(bg0_rows[:], bg0.partition_broadcast(P)).then_inc(gcn_weights_in, 16)
            sp.dma_start(bg1_rows[:], bg1.partition_broadcast(P)).then_inc(gcn_weights_in, 16)
            sp.dma_start(wg1[:], Wg1).then_inc(gcn_weights_in, 16)
            load_x(1, 1)
            with sp.Fori(0, GROUPS // 2 - 1) as i:
                for q in range(2):
                    load_x(i * 2 + (2 + q), q)

            def piece_loads(g, q):
                if exists(g + 2):
                    if isinstance(g, int) and g < 0:
                        sp.wait_ge(ax_mm, GROUPS)
                    reach(sp, y_done, g + 1)
                    sp.dma_start(xr[q][:], x_groups[g + 2]).then_inc(x_in[q], 16)

            def piece_keys(g, q):
                if exists(g + 1):
                    r = (q + 1) % 2
                    if isinstance(g, int) and g < 1:
                        sp.wait_ge(k_zeroed, r + 1)
                    sp.wait_ge(kT_done, g + 2)
                    reach(sp, s_mm, (g - 1) * GB + GB)
                    for h in range(HEADS):
                        rows = slice(h * HEAD_DIM, (h + 1) * HEAD_DIM)
                        sp.dma_start(k_diag[r][rows, :, h, :], kT[r][rows, :, :]).then_inc(k_in[r], 16)

            def piece_store(g, q):
                if exists(g - 2):
                    sp.wait_ge(res_done, g - 1)
                    sp.dma_start(out_groups[g - 2], res[q][:]).then_inc(stored[q], 16)

            def body(g, q):
                piece_loads(g, q)
                piece_keys(g, q)
                piece_store(g, q)

            attention_schedule(sp, body)
            for q in range(2):
                sp.wait_ge(stored[q], 16 * GROUPS // 2)

        @block.gpsimd
        def _(pool):
            pool.memset(ident[:], 0.0).then_inc(zeroed, 1)
            pool.wait_ge(zeroed, 1)
            pool.affine_select(out=ident[:], in_=ident[:], compare_op=ALU.not_equal, fill=1.0, base=0,
                               pattern=[[-1, P]], channel_multiplier=1).then_inc(ident_made, 1)

            for q in range(2):
                pool.memset(k_diag[q][:], 0.0).then_inc(k_zeroed, 1)
            pool.wait_ge(job_done, ALL_JOBS)
            pool.memset(minus_half[:], -0.5).then_inc(half_made, 1)
            pool.memset(eps[:], EPS).then_inc(half_made, 1)
            pool.wait_ge(half_made, 2)

            def gather_state(g, q):
                if not exists(g):
                    return
                reach(pool, hgT_mm, g - 1)
                pool.tensor_copy(hg[q][:], state[:, :, bass.ds(g * GB, GB)].rearrange("k t b -> k b t")).then_inc(hg_done, 1)

            def rstd(g, q, mv, mv_done, var, var_done, rstd, rstd_done):
                if not exists(g):
                    return
                pool.wait_ge(mv_done, g + 1)
                pool.tensor_tensor(var[q][:], mv[q][:, :, 1], eps[:], ALU.add).then_inc(var_done, 1)
                pool.wait_ge(var_done, g + 1)
                pool.tensor_tensor(rstd[q][:], var[q][:], minus_half[:], ALU.pow).then_inc(rstd_done, 1)

            def keep_x1(g, q):
                if not exists(g):
                    return
                pool.wait_ge(x1_done, (g + 1) * GB)
                pool.tensor_copy(x1_all[:, bass.ds(g * GB, GB), :], x1[q][:]).then_inc(x1_kept, 1)

            def body(g, q):
                gather_state(g + 2, q)
                keep_x1(g + 1, (q + 1) % 2)
                rstd(g - 2, q, mv2, mv2_done, var2, var2_done, rstd2, rstd2_done)
                rstd(g + 2, q, mv1, mv1_done, var1, var1_done, rstd1, rstd1_done)

            attention_schedule(pool, body)

        @block.tensor
        def _(pe):
            pe.wait_ge(ident_made, 1)
            pe.wait_ge(adj_in, 16)
            pe.transpose(bank[:, 0, 0:P], adj_nat[:], ident[:]).then_inc(prep_pe, 1)
            pe.wait_ge(prep_act, 1)
            pe.wait_ge(gcn_weights_in, 64)
            pe.matmul(bank[:, 1, 0:P], adjT[:], bg0_rows[:], start=True, stop=True).then_inc(prep_pe, 1)
            pe.matmul(bank[:, 3, 0:P], bg1_rows[:], adjT[:], start=True, stop=True).then_inc(prep_pe, 1)
            pe.wait_ge(prep_dve, 2)

            def product(out_bank, p, k, hi, lo, x_hi, x_lo, first, last):
                pe.matmul(out_bank, lo[:, p - 1, k, :], x_hi, start=first, stop=False)
                pe.matmul(out_bank, hi[:, p - 1, k, :], x_lo, start=False, stop=False)
                return pe.matmul(out_bank, hi[:, p - 1, k, :], x_hi, start=False, stop=last)

            def adj_x(g, q):
                if not exists(g):
                    return
                pe.wait_ge(x_in[q], g * 8 + (16 - 8 * q))
                reach(pe, ax_copied, g)
                for b in range(GB):
                    mm = pe.matmul(bank[:, AX_BANK, b * P:(b + 1) * P], xr[q][:, b, :], adjT[:], start=True, stop=True)
                mm.then_inc(ax_mm, 1)

            def adj_h(g, q):
                if not exists(g):
                    return
                pe.wait_ge(h0_done, g + 1)
                reach(pe, ah_copied, g)
                for b in range(GB):
                    mm = pe.matmul(bank[:, AH_BANK, b * P:(b + 1) * P], h0[q][:, b, :], adjT[:], start=True, stop=True)
                mm.then_inc(ah_mm, 1)

            def times_wg0(g, q):
                if not exists(g):
                    return
                pe.wait_ge(ax_copied, g + 1)
                reach(pe, pre0_done, g)
                for b in range(GB):
                    mm = pe.matmul(bank[:, XW_BANK, b * P:(b + 1) * P], ax[q][:, b * P:(b + 1) * P], wg0[:], start=True, stop=True)
                mm.then_inc(xw_mm, 1)

            def times_wg1(g, q):
                if not exists(g):
                    return
                pe.wait_ge(ah_copied, g + 1)
                reach(pe, pre1_done, g)
                pe.matmul(bank[:, HW_BANK, :], wg1[:], ah[q][:], start=True, stop=True).then_inc(hw_mm, 1)

            def pass1_gates(g, q):
                if not exists(g):
                    return
                if isinstance(g, int) and g == 0:
                    pe.wait_ge(w_lo_done, 1)
                    pe.wait_ge(bias_done, 1)
                pe.wait_ge(lo1_done, g + 1)
                reach(pe, gate1_done, g * 3)
                for n, k in enumerate(gates_of(0)):
                    product(bank[:, GATE1_BANK[n], :], 1, k, wih_hi, wih_lo, h1_hi[q][:], h1_lo[q][:], True,
                            True).then_inc(gate1_mm, 1)

            def turn_weights(g):
                for n in weight_quads(g):
                    raw, p = quads[n][0], quads[n][3]
                    if n == 0:
                        pe.wait_ge(lstm_weights_in, 16 * 4)
                        pe.wait_ge(bias_sum, 1)
                        pe.transpose(bank[:, W_BANK, 0:4 * MAX_SKIP], b_sum[:],
                                     ident[0:4 * MAX_SKIP, 0:4 * MAX_SKIP]).then_inc(bias_mm, 1)
                        pe.wait_ge(bias_done, 1)
                    reach(pe, w_lo_done, n)
                    for k in QUARTERS:
                        mm = pe.transpose(bank[:, W_BANK, k * P:(k + 1) * P], raw[:, p, k, :], ident[:])
                    mm.then_inc(wT_mm, 1)

            def graph_body(g, q):
                r = (q + 1) % 2
                adj_x(g, q)
                turn_weights(g)
                pass1_gates(g - 3, r)
                adj_h(g - 1, r)
                times_wg0(g, q)
                times_wg1(g - 1, r)

            graph_schedule(pe, graph_body)

            pe.wait_ge(w_lo_done, QUADS)
            pe.wait_ge(pass1_done, GROUPS)

            def job(j):
                p = j.p
                if isinstance(j.pair, int) and j.pair == 0 and j.step == 0 and p > 2:
                    pe.wait_ge(job_done, START[p][0] - 2 * (p - 1))
                if not (isinstance(j.number, int) and j.number < 2):
                    pe.wait_ge(gate_done, j.gates - j.gates_of_last)
                x_hi, x_lo = (window(s, j) for s in (state_hi, state_lo))
                gates = gates_of(j.step)
                outs = {k: columns(bank[:, j.turn * 4 + k, :], p) for k in gates}
                for k in gates:
                    mm = product(outs[k], p, k, wih_hi, wih_lo, x_hi, x_lo, True, j.step == 0)
                    if j.step == 0:
                        mm.then_inc(gate_mm, 1)
                if j.step > 0:
                    pe.wait_ge(job_done, j.before)
                    h_hi, h_lo = (columns(s[j.side], p) for s in (hid_hi, hid_lo))
                    for k in gates:
                        product(outs[k], p, k, whh_hi, whh_lo, h_hi, h_lo, False, True).then_inc(gate_mm, 1)

            lstm_schedule(pe, job)

            def piece_hgT(g, q):
                if not exists(g):
                    return
                pe.wait_ge(hg_done, g + 1)
                reach(pe, x1T_done, g)
                for b in range(GB):
                    mm = pe.transpose(bank[:, HG_BANK, b * P:(b + 1) * P], hg[q][:, b, :], ident[:])
                mm.then_inc(hgT_mm, 1)

            def piece_x1T(g, q):
                if not exists(g):
                    return
                pe.wait_ge(x1_done, (g + 1) * GB)
                for b in range(GB):
                    mm = pe.transpose(bank[:, HG_BANK, b * P:(b + 1) * P], x1[q][:, b, :], ident[:])
                mm.then_inc(x1T_mm, 1)

            def piece_qk(g, q):
                if not exists(g):
                    return
                if isinstance(g, int) and g == 0:
                    pe.wait_ge(qkv_weights_in, 16)
                pe.wait_ge(x1T_done, g + 1)
                reach(pe, scaled_done, g - 2)
                pe.matmul(bank[:, K_BANK, :], wqkv[:, DIM:2 * DIM], x1T[q][:], start=True, stop=True).then_inc(k_mm, 1)
                reach(pe, v_done, g)
                pe.matmul(bank[:, Q_BANK, :], wqkv[:, 0:DIM], x1T[q][:], start=True, stop=True).then_inc(q_mm, 1)

            def piece_v(g, q):
                if not exists(g):
                    return
                pe.wait_ge(qT_done, g + 1)
                for b in range(GB):
                    mm = pe.matmul(bank[:, Q_BANK, b * P:(b + 1) * P], x1T[q][:, b * P:(b + 1) * P],
                                   wqkv[:, 2 * DIM:3 * DIM], start=True, stop=True)
                mm.then_inc(v_mm, 1)

            def piece_o(g, q):
                if not exists(g):
                    return
                pe.wait_ge(oT_done, g + 1)
                reach(pe, kT_done, g + 3 if not isinstance(g, int) else min(g + 3, GROUPS))
                for b in range(GB):
                    mm = pe.transpose(bank[:, K_BANK, b * P:(b + 1) * P], oT[q][:, b * P:(b + 1) * P], ident[:])
                mm.then_inc(o_mm, 1)

            def scores(g, q, b):
                if not exists(g):
                    return
                n = g * GB + b
                if b == 0:
                    pe.wait_ge(k_in[q], g * 32 + (64 - 32 * q))
                reach(pe, exp_done, n - 1)
                if isinstance(g, int) and g == 0 and b == 0:
                    pe.wait_ge(mask_made, 1)
                    pe.wait_ge(ident_bf_made, 1)
                out_bank = bank[:, S_BANK[b % 2], :].rearrange("i (h j) -> i h j", h=HEADS)
                pe.matmul(out_bank, qT[q][:, b * P:(b + 1) * P], k_diag[q][:, b, :, :], start=True, stop=False)
                pe.matmul(out_bank, ident_bf[:], mask[:].to_broadcast([P, HEADS, P]), start=False, stop=True).then_inc(s_mm, 1)

            def turn_probs(g, b):
                if not exists(g):
                    return
                n = g * GB + b
                pe.wait_ge(exp_done, n + 1)
                reach(pe, pT_done, n - 1)
                for h in range(HEADS):
                    mm = pe.transpose(bank[:, PT_BANK[b % 2], h * P:(h + 1) * P], probs[b % 2][:, h, :], ident[:])
                mm.then_inc(pT_mm, 1)

            def values(g, q, b):
                if not exists(g):
                    return
                n = g * GB + b
                pe.wait_ge(pT_done, n + 1)
                if b == 0:
                    pe.wait_ge(v_done, g + 1)
                    reach(pe, oT_done, g)
                for h in range(HEADS):
                    rows = slice(h * HEAD_DIM, (h + 1) * HEAD_DIM)
                    mm = pe.matmul(bank[rows, O_BANK, b * P:(b + 1) * P], v[q][:, b, rows], probsT[b % 2][:, h, :],
                                   start=True, stop=True)
                mm.then_inc(pv_mm, 1)

            def body(g, q):
                r = (q + 1) % 2
                scores(g, q, 0)
                piece_x1T(g + 1, r)
                turn_probs(g - 1, 2)
                values(g - 1, r, 1)
                scores(g, q, 1)
                turn_probs(g - 1, 3)
                piece_hgT(g + 2, q)
                piece_qk(g + 1, r)
                values(g - 1, r, 2)
                scores(g, q, 2)
                turn_probs(g, 0)
                piece_v(g + 1, r)
                values(g - 1, r, 3)
                scores(g, q, 3)
                turn_probs(g, 1)
                piece_o(g - 1, r)
                values(g, q, 0)

            attention_schedule(pe, body)

        @block.scalar
        def _(act):
            act.dma_start(wih_raw, Wih.rearrange("p (q r) k -> r p q k", r=P)).then_inc(lstm_weights_in, 16)
            act.dma_start(whh_raw, Whh.rearrange("p (q r) k -> r p q k", r=P)).then_inc(lstm_weights_in, 16)
            act.dma_start(b_raw[:, 0, :], bih.rearrange("p (q r) -> (p q) r", r=P)).then_inc(lstm_weights_in, 16)
            act.dma_start(b_raw[:, 1, :], bhh.rearrange("p (q r) -> (p q) r", r=P)).then_inc(lstm_weights_in, 16)
            act.dma_start(wqkv[:], Wqkv).then_inc(qkv_weights_in, 16)
            act.wait_ge(prep_pe, 1)
            act.copy(adjT[:], bank[:, 0, 0:P]).then_inc(prep_act, 1)
            act.wait_ge(ident_made, 1)
            act.copy(ident_bf[:], ident[:]).then_inc(ident_bf_made, 1)

            def copy_ax(g, q):
                if not exists(g):
                    return
                act.wait_ge(ax_mm, g + 1)
                reach(act, xw_mm, g - 1)
                act.copy(ax[q][:], bank[:, AX_BANK, :]).then_inc(ax_copied, 1)

            def relu0(g, q):
                if not exists(g):
                    return
                act.wait_ge(pre0_done, g + 1)
                reach(act, ah_mm, g - 1)
                act.activation(h0[q][:], pre0[q][:], ACT.Relu).then_inc(h0_done, 1)

            def copy_ah(g, q):
                if not exists(g):
                    return
                act.wait_ge(ah_mm, g + 1)
                reach(act, hw_mm, g - 1)
                act.copy(ah[q][:], bank[:, AH_BANK, :]).then_inc(ah_copied, 1)

            def relu1(g, q):
                if not exists(g):
                    return
                act.wait_ge(pre1_done, g + 1)
                reach(act, gate1_mm, (g - 1) * 3)
                act.activation(h1_hi[q][:], pre1[q][:], ACT.Relu).then_inc(hi1_done, 1)

            def pass1_gates(g, q):
                if not exists(g):
                    return
                for n, k in enumerate(gates_of(0)):
                    act.wait_ge(gate1_mm, g * 3 + (n + 1))
                    act.activation(gate1[q][n][:], bank[:, GATE1_BANK[n], :], GATE_FUNCTION[k],
                                   bias=gate_bias[:, k:k + 1]).then_inc(gate1_done, 1)

            def pass1_tanh(g, q):
                if not exists(g):
                    return
                act.wait_ge(cell1_done, g + 1)
                act.activation(cell1_tanh[q][:], cell1[q][:], ACT.Tanh).then_inc(tanh1_done, 1)

            def split_weights(g):
                for n in weight_quads(g):
                    hi, p = quads[n][1], quads[n][3]
                    if n == 0:
                        act.wait_ge(bias_mm, 1)
                        act.copy(gate_bias[:], bank[:, W_BANK, 0:4 * MAX_SKIP]).then_inc(bias_done, 1)
                        act.wait_ge(bias_done, 1)
                    act.wait_ge(wT_mm, n + 1)
                    act.copy(hi[:, p, :, :], bank[:, W_BANK, :].rearrange("k (q r) -> k q r", q=4)).then_inc(w_hi_done, 1)

            def graph_body(g, q):
                r = (q + 1) % 2
                relu1(g - 2, q)
                copy_ax(g, q)
                split_weights(g)
                pass1_gates(g - 3, r)
                copy_ah(g - 1, r)
                pass1_tanh(g - 3, r)
                relu0(g, q)

            graph_schedule(act, graph_body)

            def job(j):
                p = j.p
                if not (isinstance(j.number, int) and j.number < 2):
                    act.wait_ge(hid_done, j.number - 1)
                for n, k in enumerate(gates_of(j.step)):
                    act.wait_ge(gate_mm, j.gates + (n + 1))
                    act.activation(columns(gate[j.turn][k], p), columns(bank[:, j.turn * 4 + k, :], p), GATE_FUNCTION[k],
                                   bias=gate_bias[:, 4 * (p - 1) + k:4 * (p - 1) + k + 1]).then_inc(gate_done, 1)
                act.wait_ge(cell_done, j.number + 1)
                act.activation(columns(cell_tanh[j.turn], p), columns(cell[j.side], p), ACT.Tanh).then_inc(tanh_done, 1)

            lstm_schedule(act, job)

            def copy_x1T(g, q):
                if not exists(g):
                    return
                act.wait_ge(x1T_mm, g + 1)
                reach(act, v_mm, g - 1)
                act.copy(x1T[q][:], bank[:, HG_BANK, :]).then_inc(x1T_done, 1)

            def copy_qT(g, q):
                if not exists(g):
                    return
                act.wait_ge(q_mm, g + 1)
                reach(act, s_mm, (g - 1) * GB)
                act.mul(qT[q][:], bank[:, Q_BANK, :], HEAD_DIM ** -0.5).then_inc(qT_done, 1)

            def copy_kT(g, q):
                if not exists(g):
                    return
                act.wait_ge(k_mm, g + 1)
                reach(act, k_in[q], g * 32 - 32 * q)
                act.copy(kT[q][:], bank[:, K_BANK, :].rearrange("k (b t) -> k b t", b=GB)).then_inc(kT_done, 1)

            def exponentials(g, q, b):
                if not exists(g):
                    return
                n = g * GB + b
                act.wait_ge(max_done, n + 1)
                reach(act, pT_mm, n - 1)
                if b == 0:
                    reach(act, rden_done, g - 1)
                for h in range(HEADS):
                    e = act.activation(probs[b % 2][:, h, :], bank[:, S_BANK[b % 2], h * P:(h + 1) * P], ACT.Exp,
                                       bias=neg_max[b % 2][:, h:h + 1], accum_out=den[q][:, b * HEADS + h:b * HEADS + h + 1])
                e.then_inc(exp_done, 1)

            def copy_pT(g, b):
                if not exists(g):
                    return
                n = g * GB + b
                act.wait_ge(pT_mm, n + 1)
                reach(act, pv_mm, n - 1)
                act.copy(probsT[b % 2][:], bank[:, PT_BANK[b % 2], :].rearrange("j (h i) -> j h i", h=HEADS)).then_inc(pT_done, 1)

            def body(g, q):
                r = (q + 1) % 2
                copy_x1T(g + 1, r)
                exponentials(g, q, 0)
                copy_pT(g - 1, 2)
                exponentials(g, q, 1)
                copy_kT(g + 1, r)
                copy_qT(g + 1, r)
                copy_pT(g - 1, 3)
                exponentials(g, q, 2)
                copy_pT(g, 0)
                exponentials(g, q, 3)
                copy_pT(g, 1)

            attention_schedule(act, body)

        @block.vector
        def _(dve):
            dve.wait_ge(adj_in, 16)
            dve.tensor_scalar(mask[:, 0, :], adj_nat[:], 0.0, MASKED, ALU.is_equal, ALU.mult).then_inc(mask_made, 1)
            dve.wait_ge(prep_pe, 3)
            dve.tensor_copy(bias0[:, 0, :], bank[:, 1, 0:P]).then_inc(prep_dve, 1)
            dve.tensor_copy(bias1[:, 0, :], bank[:, 3, 0:P]).then_inc(prep_dve, 1)
            dve.wait_ge(prep_dve, 2)
            dve.wait_ge(lstm_weights_in, 16 * 4)
            dve.tensor_tensor(b_sum[:], b_raw[:, 0, :], b_raw[:, 1, :], ALU.add).then_inc(bias_sum, 1)

            def add0(g, q):
                if not exists(g):
                    return
                dve.wait_ge(xw_mm, g + 1)
                reach(dve, h0_done, g - 1)
                dve.tensor_tensor(pre0[q][:], bank[:, XW_BANK, :].rearrange("t (b d) -> t b d", b=GB),
                                  bias0[:].to_broadcast([P, GB, DIM]), ALU.add).then_inc(pre0_done, 1)

            def add1(g, q):
                if not exists(g):
                    return
                dve.wait_ge(hw_mm, g + 1)
                reach(dve, lo1_done, g - 1)
                dve.tensor_tensor(pre1[q][:].rearrange("k (b t) -> k b t", b=GB),
                                  bank[:, HW_BANK, :].rearrange("k (b t) -> k b t", b=GB),
                                  bias1[:].to_broadcast([P, GB, STEPS]), ALU.add).then_inc(pre1_done, 1)

            def low1(g, q):
                if not exists(g):
                    return
                dve.wait_ge(hi1_done, g + 1)
                dve.scalar_tensor_tensor(out=h1_lo[q][:], in0=pre1[q][:], scalar=0.0, in1=h1_hi[q][:].bitcast(F32),
                                         op0=ALU.max, op1=ALU.subtract).then_inc(lo1_done, 1)

            def pass1_cell(g, q):
                if not exists(g):
                    return
                dve.wait_ge(gate1_done, g * 3 + 2)
                dve.tensor_tensor(cell1[q][:], gate1[q][0][:], gate1[q][1][:], ALU.mult).then_inc(cell1_done, 1)

            def group_states(buffer, g):
                return buffer[:, :, bass.ds(g * GB, GB)].rearrange("k t b -> k b t")

            def pass1_hidden(g, q):
                if not exists(g):
                    return
                dve.wait_ge(tanh1_done, g + 1)
                dve.wait_ge(gate1_done, g * 3 + 3)
                dve.tensor_tensor(group_states(state, g), gate1[q][2][:].rearrange("k (b t) -> k b t", b=GB),
                                  cell1_tanh[q][:].rearrange("k (b t) -> k b t", b=GB), ALU.mult).then_inc(hid1_done, 1)

            def pass1_hi(g, q):
                if not exists(g):
                    return
                dve.wait_ge(hid1_done, g + 1)
                dve.tensor_copy(group_states(state_hi, g), group_states(state, g)).then_inc(hid1_hi_done, 1)

            def pass1_lo(g, q):
                if not exists(g):
                    return
                dve.wait_ge(hid1_hi_done, g + 1)
                dve.tensor_tensor(group_states(state_lo, g), group_states(state, g), group_states(state_hi, g).bitcast(F32),
                                  ALU.subtract).then_inc(pass1_done, 1)

            def split_weights(g):
                for n in weight_quads(g):
                    _, hi, lo, p = quads[n]
                    dve.wait_ge(w_hi_done, n + 1)
                    dve.tensor_tensor(lo[:, p, :, :], bank[:, W_BANK, :].rearrange("k (q r) -> k q r", q=4),
                                      hi[:, p, :, :].bitcast(F32), ALU.subtract).then_inc(w_lo_done, 1)

            def graph_body(g, q):
                r = (q + 1) % 2
                add1(g - 2, q)
                pass1_hi(g - 4, q)
                low1(g - 2, q)
                pass1_lo(g - 4, q)
                split_weights(g)
                pass1_cell(g - 3, r)
                add0(g, q)
                pass1_hidden(g - 3, r)

            graph_schedule(dve, graph_body)

            def job(j):
                p = j.p
                i_, f_, g_, o_ = (columns(gate[j.turn][k], p) for k in QUARTERS)
                c = columns(cell[j.side], p)
                dve.wait_ge(gate_done, j.gates + 2)
                if j.step == 0:
                    dve.tensor_tensor(c, i_, g_, ALU.mult).then_inc(cell_done, 1)
                else:
                    new = columns(in_cell[j.turn], p)
                    dve.tensor_tensor(new, i_, g_, ALU.mult).then_inc(in_cell_done, 1)
                    dve.wait_ge(gate_done, j.gates + 3)
                    dve.tensor_tensor(c, f_, c, ALU.mult).then_inc(kept_done, 1)
                    dve.wait_ge(in_cell_done, j.later + 1)
                    dve.wait_ge(kept_done, j.later + 1)
                    dve.tensor_tensor(c, c, new, ALU.add).then_inc(cell_done, 1)
                if j.step == p - 1:
                    full, hi, lo = (window(s, j) for s in (state, state_hi, state_lo))
                else:
                    full, hi, lo = (columns(s[j.side], p) for s in (hid, hid_hi, hid_lo))
                dve.wait_ge(tanh_done, j.number + 1)
                dve.tensor_tensor(full, o_, columns(cell_tanh[j.turn], p), ALU.mult).then_inc(hid_done, 1)
                dve.wait_ge(hid_done, j.number + 1)
                dve.tensor_copy(hi, full).then_inc(hid_hi_done, 1)
                dve.wait_ge(hid_hi_done, j.number + 1)
                dve.tensor_tensor(lo, full, hi.bitcast(F32), ALU.subtract).then_inc(job_done, 1)

            lstm_schedule(dve, job)

            def maximum(g, b):
                if not exists(g):
                    return
                n = g * GB + b
                dve.wait_ge(s_mm, n + 1)
                reach(dve, exp_done, n - 1)
                dve.tensor_reduce(neg_max[b % 2][:], bank[:, S_BANK[b % 2], :].rearrange("i (h j) -> i h j", h=HEADS),
                                  AX_X, ALU.max, negate=True).then_inc(max_done, 1)

            def partial_stats(source, stats, bn_done):
                for b in range(GB):
                    last = dve.bn_stats(stats[:, b, :], source[:, b, :])
                last.then_inc(bn_done, 1)

            def mean_var(g, stats, mv, mv_done):
                if not exists(g):
                    return
                for b in range(GB):
                    last = dve.bn_aggr(mv[:, b, :], stats[:, b, :])
                last.then_inc(mv_done, 1)

            def stats_ready(g, bn_done):
                if exists(g):
                    dve.wait_ge(bn_done, g + 1)

            def residual1(g, q):
                if not exists(g):
                    return
                dve.wait_ge(hgT_mm, g + 1)
                dve.wait_ge(x_in[q], g * 8 + (16 - 8 * q) + 16 * (GROUPS // 2))
                reach(dve, x1_done, (g - 1) * GB)
                dve.tensor_tensor(y[q][:], bank[:, HG_BANK, :].rearrange("t (b d) -> t b d", b=GB), xr[q][:],
                                  ALU.add).then_inc(y_done, 1)
                dve.wait_ge(y_done, g + 1)
                partial_stats(y[q], stats1[q], bn1_done)

            def norm1(g, q):
                if not exists(g):
                    return
                dve.wait_ge(rstd1_done, g + 1)
                reach(dve, x1_kept, g - 1)
                reach(dve, x1T_mm, g - 1)
                for b in range(GB):
                    dve.tensor_scalar(x1[q][:, b, :], y[q][:, b, :], mv1[q][:, b, 0:1], rstd1[q][:, b:b + 1],
                                      ALU.subtract, ALU.mult).then_inc(x1_done, 1)

            def copy_v(g, q):
                if not exists(g):
                    return
                dve.wait_ge(v_mm, g + 1)
                reach(dve, pv_mm, (g - 1) * GB)
                dve.tensor_copy(v[q][:], bank[:, Q_BANK, :].rearrange("t (b d) -> t b d", b=GB)).then_inc(v_done, 1)

            def copy_oT(g, q):
                if not exists(g):
                    return
                dve.wait_ge(pv_mm, (g + 1) * GB)
                dve.tensor_copy(oT[q][:], bank[:, O_BANK, :]).then_inc(oT_done, 1)

            def reciprocal(g, q):
                if not exists(g):
                    return
                dve.wait_ge(exp_done, (g + 1) * GB)
                dve.reciprocal(rden[q][:, :, 0], den[q][:]).then_inc(rden_done, 1)

            def residual2(g, q):
                if not exists(g):
                    return
                dve.wait_ge(o_mm, g + 1)
                dve.wait_ge(rden_done, g + 1)
                dve.tensor_tensor(z[q][:].rearrange("t b (h d) -> t (b h) d", h=HEADS),
                                  bank[:, K_BANK, :].rearrange("t (c d) -> t c d", d=HEAD_DIM),
                                  rden[q][:].to_broadcast([P, GB * HEADS, HEAD_DIM]), ALU.mult).then_inc(scaled_done, 1)
                dve.wait_ge(scaled_done, g + 1)
                dve.wait_ge(x1_kept, g + 1)
                dve.tensor_tensor(z[q][:], z[q][:], x1_all[:, bass.ds(g * GB, GB), :], ALU.add).then_inc(z_done, 1)
                dve.wait_ge(z_done, g + 1)
                partial_stats(z[q], stats2[q], bn2_done)

            def norm2(g, q):
                if not exists(g):
                    return
                dve.wait_ge(rstd2_done, g + 1)
                reach(dve, stored[q], g * 8 - 8 * q)
                for b in range(GB):
                    last = dve.tensor_scalar(res[q][:, b, :], z[q][:, b, :], mv2[q][:, b, 0:1], rstd2[q][:, b:b + 1],
                                             ALU.subtract, ALU.mult)
                last.then_inc(res_done, 1)

            def body(g, q):
                r = (q + 1) % 2
                maximum(g, 0)
                reciprocal(g - 1, r)
                residual2(g - 2, q)
                stats_ready(g - 2, bn2_done)
                maximum(g, 1)
                mean_var(g - 2, stats2[q], mv2[q], mv2_done)
                residual1(g + 2, q)
                stats_ready(g + 2, bn1_done)
                maximum(g, 2)
                mean_var(g + 2, stats1[q], mv1[q], mv1_done)
                norm2(g - 2, q)
                copy_oT(g - 1, r)
                maximum(g, 3)
                copy_v(g + 1, r)
                norm1(g + 2, q)

            attention_schedule(dve, body)


_INPUTS = ("x", "adj", "L0_gnn_Wg0", "L0_gnn_bg0", "L0_gnn_Wg1", "L0_gnn_bg1", "L0_gnn_Wih", "L0_gnn_Whh",
           "L0_gnn_bih", "L0_gnn_bhh", "L1_gnn_W")


def kernel(**inputs):
    import numpy as np
    import concourse.bacc as bacc
    from concourse.bass_utils import run_bass_kernel_spmd

    nc = bacc.Bacc("TRN2", target_bir_lowering=False, num_devices=1)
    arrays, args = {}, []
    for name in _INPUTS:
        a = np.ascontiguousarray(inputs[name])
        arrays[f"in_{name}"] = a
        args.append(nc.dram_tensor(f"in_{name}", a.shape, mybir.dt.from_np(a.dtype), kind="ExternalInput").ap())
    args.append(nc.dram_tensor("out_dram", (BATCH, STEPS, DIM), F32, kind="ExternalOutput").ap())
    build(nc, *args)
    done = run_bass_kernel_spmd(nc, [arrays], core_ids=[0])
    return done.results[0]["out_dram"]
```

```python
from contextlib import ExitStack

import concourse.bass as bass
from concourse import mybir

ALU = mybir.AluOpType
ACT = mybir.ActivationFunctionType
AX_X = mybir.AxisListType.X
F32 = mybir.dt.float32
F32R = mybir.dt.float32r
BF16 = mybir.dt.bfloat16

BATCH, STEPS, DIM = 64, 128, 128
P = 128
GB = 4
GROUPS = BATCH // GB
HEADS = 4
HEAD_DIM = DIM // HEADS
MAX_SKIP = 4
EPS = 1e-5
MASKED = -1e30
QUARTERS = (0, 1, 2, 3)
GATE_I, GATE_F, GATE_G, GATE_O = QUARTERS
GATE_FUNCTION = {GATE_I: ACT.Sigmoid, GATE_F: ACT.Sigmoid, GATE_G: ACT.Tanh, GATE_O: ACT.Sigmoid}

WINDOWS = {p: STEPS // p for p in range(2, MAX_SKIP + 1)}
CHUNK = {2: 8, 3: 8, 4: 16}
PAIRS = {p: BATCH // CHUNK[p] // 2 for p in CHUNK}
assert all(WINDOWS[p] * CHUNK[p] <= 512 and PAIRS[p] * 2 * CHUNK[p] == BATCH for p in CHUNK)


def gates_of(step):
    return (GATE_I, GATE_G, GATE_O) if step == 0 else (GATE_F, GATE_I, GATE_G, GATE_O)


class Job:

    def __init__(self, p, pair, step, side, number, gates, later, lasts, split, before, turn, gates_of_last, shared=False):
        self.p, self.pair, self.step, self.side = p, pair, step, side
        self.number, self.gates, self.later, self.lasts = number, gates, later, lasts
        self.split, self.before = split, before
        self.turn, self.gates_of_last, self.shared = turn, gates_of_last, shared
        self.banks = 4 if shared else 4 * turn


LAST_PAIR = {p: PAIRS[p] - 1 for p in PAIRS}
START = {2: (2, 6, 0, 0)}
for _p in range(3, MAX_SKIP + 1):
    START[_p] = tuple(n + PAIRS[_p - 1] * m for n, m in
                      zip(START[_p - 1], (2 * (_p - 1), 8 * (_p - 2) + 6, 2 * (_p - 2), 2)))
ALL_JOBS = sum(2 * p * PAIRS[p] for p in PAIRS)
ALL_GATES = sum((8 * (p - 1) + 6) * PAIRS[p] for p in PAIRS)


def first_jobs():
    return [Job(2, 0, 0, side, side, 3 * side, 0, 0, side, 0, side, 3) for side in range(2)]


def body_jobs(p, pair):
    last = isinstance(pair, int) and pair == LAST_PAIR[p]
    final = last and p == MAX_SKIP
    after = (p + 1, 0) if last else (p, pair + 1)
    order = [(p, pair, step, side) for step in range(1, p - 1) for side in range(2)]
    order.append((p, pair, p - 1, 0))
    if not final:
        order.append((*after, 0, 0))
    order.append((p, pair, p - 1, 1))
    if not final:
        order.append((*after, 0, 1))
    place = {0: (-3, -1), 1: (-1, 0)}
    if p == 2 and isinstance(pair, int) and pair == 0:
        place[0] = (-2, 0)
    jobs0, gates0, later0, lasts0 = START[p]
    gates, later, lasts, gates_of_last, jobs = 0, 0, 0, 3, []
    for n, (p_, pair_, step, side) in enumerate(order):
        n_before, lasts_before = place[side]
        jobs.append(Job(
            p_, pair_, step, side, number=pair * (2 * p) + (jobs0 + n), gates=pair * (8 * (p - 1) + 6) + (gates0 + gates),
            later=pair * (2 * (p - 1)) + (later0 + later), lasts=pair * 2 + (lasts0 + lasts),
            split=pair * (2 * p - 2) + (jobs0 + n - lasts0 - lasts),
            before=pair * (2 * p - 2) + (jobs0 + n_before - lasts0 - lasts_before + 1),
            turn=n % 2, gates_of_last=gates_of_last, shared=final and n >= 2))
        if step > 0:
            place[side] = (n, lasts)
            later += 1
            lasts += step == p - 1
        gates_of_last = len(gates_of(step))
        gates += gates_of_last
    return jobs


def reach(engine, semaphore, count):
    if not isinstance(count, int) or count > 0:
        engine.wait_ge(semaphore, count)


def build(nc, x, adj, Wg0, bg0, Wg1, bg1, Wih, Whh, bih, bhh, Wqkv, out):
    x_groups = x.rearrange("(g b) t d -> g t b d", b=GB)
    out_groups = out.rearrange("(g b) t d -> g t b d", b=GB)

    with ExitStack() as ctx:
        def sem(name):
            return ctx.enter_context(nc.semaphore(name))

        def sb(stack, name, shape, dtype=F32):
            return stack.enter_context(nc.sbuf_tensor(name, shape, dtype))

        bank = ctx.enter_context(nc.psum_tensor("bank", [P, 8, 512], F32))

        ident = sb(ctx, "ident", [P, P])
        ident_bf = sb(ctx, "ident_bf", [P, P], BF16)
        mask = sb(ctx, "mask", [P, 1, P], BF16)
        wqkv = sb(ctx, "wqkv", [P, 3 * DIM])
        xr = [sb(ctx, f"xr{q}", [P, GB, DIM]) for q in range(2)]
        state = sb(ctx, "state", [P, STEPS, BATCH])
        gate_bias = sb(ctx, "gate_bias", [P, 4 * MAX_SKIP])
        k_diag = [sb(ctx, "k_diag0", [P, 2 * GB, HEADS, STEPS], F32R)]

        def weights(stack, name, p):
            return sb(stack, f"{name}{p}", [P, 4, P], F32R)

        early_mem = ExitStack()
        wih_hi = [weights(early_mem, "wih_hi", p) for p in range(1, MAX_SKIP)]
        wih_lo = [weights(early_mem, "wih_lo", p) for p in range(1, MAX_SKIP)]
        whh_hi = [weights(early_mem, "whh_hi", p) for p in range(2, MAX_SKIP)]
        whh_lo = [weights(early_mem, "whh_lo", p) for p in range(2, MAX_SKIP)]
        cell1_tanh = [sb(early_mem, f"cell1_tanh{q}", [P, GB * STEPS]) for q in range(2)]
        cell1 = [sb(early_mem, f"cell1{q}", [P, GB * STEPS]) for q in range(2)]
        gate1 = [[sb(early_mem, f"gate1{q}{k}", [P, GB * STEPS]) for k in range(3)] for q in range(2)]
        early_mem.close()

        hg = [sb(ctx, f"hg{q}", [P, GB, STEPS]) for q in range(2)]
        y = [sb(ctx, f"y{q}", [P, GB, DIM]) for q in range(2)]
        x1 = [sb(ctx, f"x1{q}", [P, GB, DIM]) for q in range(2)]
        x1T = [sb(ctx, f"x1T{q}", [P, GB * STEPS]) for q in range(2)]
        q_hi = [sb(ctx, "q_hi0", [P, GB * STEPS], F32R)]
        q_lo = [sb(ctx, "q_lo0", [P, GB * STEPS], F32R)]
        k_parts = [sb(ctx, "k_parts0", [P, 2 * GB, STEPS], F32R)]
        k_diag.append(sb(ctx, "k_diag1", [P, 2 * GB, HEADS, STEPS], F32R))
        stats1 = [sb(ctx, f"stats1{q}", [P, GB, 6]) for q in range(2)]
        mv1 = [sb(ctx, f"mv1{q}", [P, GB, 2]) for q in range(2)]
        var1 = [sb(ctx, f"var1{q}", [P, GB]) for q in range(2)]
        rstd1 = [sb(ctx, f"rstd1{q}", [P, GB]) for q in range(2)]
        minus_half = sb(ctx, "minus_half", [P, GB])
        eps = sb(ctx, "eps", [P, GB])
        exp_eps = sb(ctx, "exp_eps", [P, GB])

        lstm_mem = ExitStack()
        wih_hi.append(weights(lstm_mem, "wih_hi", MAX_SKIP))
        wih_lo.append(weights(lstm_mem, "wih_lo", MAX_SKIP))
        whh_hi.append(weights(lstm_mem, "whh_hi", MAX_SKIP))
        whh_lo.append(weights(lstm_mem, "whh_lo", MAX_SKIP))
        state_hi = sb(lstm_mem, "state_hi", [P, STEPS, BATCH], F32R)
        state_lo = sb(lstm_mem, "state_lo", [P, STEPS, BATCH], F32R)

        gcn_mem = ExitStack()
        adj_nat = sb(gcn_mem, "adj_nat", [P, P])
        adjT = sb(gcn_mem, "adjT", [P, P])
        wg0 = sb(gcn_mem, "wg0", [P, DIM])
        wg1 = sb(gcn_mem, "wg1", [P, DIM])
        wg1_hi = sb(gcn_mem, "wg1_hi", [P, DIM], F32R)
        wg1_lo = sb(gcn_mem, "wg1_lo", [P, DIM], F32R)
        bg0_rows = sb(gcn_mem, "bg0_rows", [P, DIM])
        bg1_rows = sb(gcn_mem, "bg1_rows", [P, DIM])
        bias0 = sb(gcn_mem, "bias0", [P, 1, DIM])
        bias1 = sb(gcn_mem, "bias1", [P, 1, P])
        raw = state[:].rearrange("k t b -> k (t b)")[:, 0:2 * MAX_SKIP * 4 * P].rearrange(
            "k (w p q r) -> k w p q r", w=2, p=MAX_SKIP, q=4)
        wih_raw, whh_raw = raw[:, 0], raw[:, 1]
        b_raw = sb(gcn_mem, "b_raw", [4 * MAX_SKIP, 2, P])
        b_sum = sb(gcn_mem, "b_sum", [4 * MAX_SKIP, P])
        ax = [sb(gcn_mem, f"ax{q}", [P, GB * STEPS]) for q in range(2)]
        pre0 = [sb(gcn_mem, f"pre0{q}", [P, GB, DIM]) for q in range(2)]
        h0 = [sb(gcn_mem, f"h0{q}", [P, GB, DIM]) for q in range(2)]
        ah_hi = [sb(gcn_mem, f"ah_hi{q}", [P, GB * STEPS], F32R) for q in range(2)]
        ah_lo = [sb(gcn_mem, f"ah_lo{q}", [P, GB * STEPS], F32R) for q in range(2)]
        pre1 = [sb(gcn_mem, f"pre1{q}", [P, GB * STEPS]) for q in range(2)]
        h1_hi = [sb(gcn_mem, f"h1_hi{q}", [P, GB * STEPS], F32R) for q in range(2)]
        h1_lo = [sb(gcn_mem, f"h1_lo{q}", [P, GB * STEPS], F32R) for q in range(2)]
        gcn_mem.close()

        step_mem = ExitStack()
        N = 512
        gate = [[sb(step_mem, f"gate{q}{k}", [P, N]) for k in QUARTERS] for q in range(2)]
        in_cell = [sb(step_mem, f"in_cell{q}", [P, N]) for q in range(2)]
        cell = [sb(step_mem, f"cell{q}", [P, N]) for q in range(2)]
        cell_tanh = [sb(step_mem, f"cell_tanh{q}", [P, N]) for q in range(2)]
        hid = [sb(step_mem, f"hid{q}", [P, N]) for q in range(2)]
        hid_hi = [sb(step_mem, f"hid_hi{q}", [P, N], F32R) for q in range(2)]
        hid_lo = [sb(step_mem, f"hid_lo{q}", [P, N], F32R) for q in range(2)]
        step_mem.close()
        lstm_mem.close()

        attn_mem = ExitStack()
        ctx.enter_context(attn_mem)
        x1_all = sb(attn_mem, "x1_all", [P, BATCH, DIM])
        q_hi.append(sb(attn_mem, "q_hi1", [P, GB * STEPS], F32R))
        q_lo.append(sb(attn_mem, "q_lo1", [P, GB * STEPS], F32R))
        k_parts.append(sb(attn_mem, "k_parts1", [P, 2 * GB, STEPS], F32R))
        v = [sb(attn_mem, f"v{q}", [P, GB, DIM]) for q in range(2)]
        probs = [sb(attn_mem, f"probs{q}", [P, HEADS, STEPS]) for q in range(2)]
        probsT = [sb(attn_mem, f"probsT{q}", [P, HEADS, STEPS]) for q in range(2)]
        oT = [sb(attn_mem, f"oT{q}", [P, GB * STEPS]) for q in range(2)]
        z = [sb(attn_mem, f"z{q}", [P, GB, DIM]) for q in range(2)]
        res = [sb(attn_mem, f"res{q}", [P, GB, DIM]) for q in range(2)]
        neg_max = [sb(attn_mem, f"neg_max{q}", [P, HEADS]) for q in range(2)]
        den = [sb(attn_mem, f"den{q}", [P, GB * HEADS]) for q in range(2)]
        rden = [sb(attn_mem, f"rden{q}", [P, GB * HEADS, 1]) for q in range(2)]
        stats2 = [sb(attn_mem, f"stats2{q}", [P, GB, 6]) for q in range(2)]
        mv2 = [sb(attn_mem, f"mv2{q}", [P, GB, 2]) for q in range(2)]
        var2 = [sb(attn_mem, f"var2{q}", [P, GB]) for q in range(2)]
        rstd2 = [sb(attn_mem, f"rstd2{q}", [P, GB]) for q in range(2)]


        half_made, var1_done, var2_done = sem("half_made"), sem("var1_done"), sem("var2_done")
        adj_in, gcn_weights_in, wih_in, whh_in = sem("adj_in"), sem("gcn_weights_in"), sem("wih_in"), sem("whh_in")
        lstm_biases_in, qkv_weights_in = sem("lstm_biases_in"), sem("qkv_weights_in")
        x_in = [sem(f"x_in{q}") for q in range(2)]
        zeroed, ident_made, ident_bf_made = sem("zeroed"), sem("ident_made"), sem("ident_bf_made")
        prep_pe, adjT_done, prep_dve = sem("prep_pe"), sem("adjT_done"), sem("prep_dve")
        mask_made, wg1_hi_done, wg1_lo_done = sem("mask_made"), sem("wg1_hi_done"), sem("wg1_lo_done")
        ax_mm, ax_copied, xw_mm, pre0_done, h0_done = (sem(s) for s in ("ax_mm", "ax_copied", "xw_mm", "pre0_done", "h0_done"))
        ah_mm, ah_hi_done, ah_lo_done, hw_mm, pre1_done, hi1_done, lo1_done = (
            sem(s) for s in ("ah_mm", "ah_hi_done", "ah_lo_done", "hw_mm", "pre1_done", "hi1_done", "lo1_done"))
        wT_mm, w_hi_done, w_lo_done = sem("wT_mm"), sem("w_hi_done"), sem("w_lo_done")
        bias_sum, bias_mm, bias_done = sem("bias_sum"), sem("bias_mm"), sem("bias_done")
        gate1_mm, gate1_done, cell1_done, tanh1_done, hid1_done, hid1_hi_done, pass1_done = (
            sem(s) for s in ("gate1_mm", "gate1_done", "cell1_done", "tanh1_done", "hid1_done", "hid1_hi_done", "pass1_done"))
        gate_mm, gate_done = sem("gate_mm"), sem("gate_done")
        in_cell_done, kept_done = sem("in_cell_done"), sem("kept_done")
        cell_done, tanh_done, hid_done, hid_hi_done, hid_split, last_hi_done, last_split = (
            sem(s) for s in ("cell_done", "tanh_done", "hid_done", "hid_hi_done", "hid_split", "last_hi_done", "last_split"))
        hg_done, hgT_mm, y_done, bn1_done, mv1_done, rstd1_done, x1_done, x1_kept = (
            sem(s) for s in ("hg_done", "hgT_mm", "y_done", "bn1_done", "mv1_done", "rstd1_done", "x1_done", "x1_kept"))
        x1T_mm, x1T_done, q_mm, q_hi_done, q_lo_done, k_mm, k_hi_done, k_lo_done, v_mm, v_done = (
            sem(s) for s in ("x1T_mm", "x1T_done", "q_mm", "q_hi_done", "q_lo_done", "k_mm", "k_hi_done", "k_lo_done",
                             "v_mm", "v_done"))
        k_zeroed = sem("k_zeroed")
        k_in = [sem(f"k_in{q}") for q in range(2)]
        oT_done, o_mm, rden_done, scaled_done, z_done, bn2_done, mv2_done, rstd2_done, res_done = (
            sem(s) for s in ("oT_done", "o_mm", "rden_done", "scaled_done", "z_done", "bn2_done", "mv2_done", "rstd2_done", "res_done"))
        stored = [sem(f"stored{q}") for q in range(2)]
        s_mm, max_done, exp_done, pT_mm, pT_done, pv_mm = (
            sem(s) for s in ("s_mm", "max_done", "exp_done", "pT_mm", "pT_done", "pv_mm"))

        QUADS = 2 * MAX_SKIP - 1
        quads = [(wih_raw, wih_hi, wih_lo, p) for p in range(MAX_SKIP)] + \
                [(whh_raw, whh_hi, whh_lo, p) for p in range(MAX_SKIP - 1)]

        def group_states(buffer, g):
            return buffer[:, :, bass.ds(g * GB, GB)].rearrange("k t b -> k b t")

        def columns(buffer, p):
            return buffer[:, 0:WINDOWS[p] * CHUNK[p]].rearrange("k (w b) -> k w b", b=CHUNK[p])

        def window(buffer, j):
            n, p = CHUNK[j.p], j.p
            part = buffer[:, 0:WINDOWS[p] * p, :].rearrange("k (w s) b -> k w s b", s=p)
            return part[:, :, j.step, bass.ds(j.pair * (2 * n) + j.side * n, n)]

        HG_BANK, Q_BANK, K_BANK, O_BANK = 0, 1, 2, 3
        FIRST_HG_BANK = 4 + GATE_F
        S_BANK, PT_BANK = (4, 5), (6, 7)
        AX_BANK, XW_BANK, AH_BANK, HW_BANK, GATE1_BANK, W_BANK = 0, 1, 2, 3, (4, 5, 6), (7, 4, 5, 6)
        BIAS_BANK = (4, 5)

        def graph_schedule(engine, body):
            for g in range(4):
                body(g, g % 2)
            with engine.Fori(0, (GROUPS - 4) // 2) as i:
                for side in range(2):
                    body(i * 2 + (4 + side), side)
            for g in range(GROUPS, GROUPS + 4):
                body(g, g % 2)

        def weight_quads(g):
            if not isinstance(g, int) or g > 2:
                return ()
            return ((), (0, 1, 2), (3, 4, 5, 6))[g]

        def lstm_schedule(engine, job, between):
            for j in first_jobs():
                job(j)
            for p in range(2, MAX_SKIP + 1):
                start = 1 if p == 2 else 0
                if start:
                    for j in body_jobs(p, 0):
                        job(j)
                if LAST_PAIR[p] - start > 1:
                    with engine.Fori(start, LAST_PAIR[p]) as pair:
                        for j in body_jobs(p, pair):
                            job(j)
                else:
                    for j in body_jobs(p, start):
                        job(j)
                if p == MAX_SKIP:
                    between(-1)
                for n, j in enumerate(body_jobs(p, LAST_PAIR[p])):
                    job(j)
                    if p == MAX_SKIP:
                        between(n)

        def attention_schedule(engine, body, first):
            for g in range(first, 4):
                body(g, g % 2)
            with engine.Fori(0, (GROUPS - 6) // 2) as i:
                for side in range(2):
                    body(i * 2 + (4 + side), side)
            for g in range(GROUPS - 2, GROUPS + 2):
                body(g, g % 2)

        def after_first(g):
            return -2 if isinstance(g, int) and g == 0 else g + 1

        def exists(g):
            return not isinstance(g, int) or 0 <= g < GROUPS

        block = ctx.enter_context(nc.Block())

        @block.sync
        def _(sp):
            sp.dma_start(adj_nat[:], adj).then_inc(adj_in, 16)

            def load_x(g, q):
                reach(sp, ax_mm, g - 1)
                sp.dma_start(xr[q][:], x_groups[g]).then_inc(x_in[q], 16)

            load_x(0, 0)
            sp.dma_start(bg0_rows[:], bg0.partition_broadcast(P)).then_inc(gcn_weights_in, 16)
            sp.dma_start(bg1_rows[:], bg1.partition_broadcast(P)).then_inc(gcn_weights_in, 16)
            load_x(1, 1)
            sp.dma_start(wih_raw, Wih.rearrange("p (q r) k -> r p q k", r=P)).then_inc(wih_in, 16)
            sp.dma_start(whh_raw[:, 0:MAX_SKIP - 1], Whh[1:MAX_SKIP].rearrange("p (q r) k -> r p q k", r=P)).then_inc(whh_in, 16)
            sp.dma_start(wqkv[:], Wqkv).then_inc(qkv_weights_in, 16)
            with sp.Fori(0, GROUPS // 2 - 1) as i:
                for q in range(2):
                    load_x(i * 2 + (2 + q), q)

            def piece_loads(g, q):
                if exists(g + 2):
                    if isinstance(g, int) and g < 0:
                        sp.wait_ge(ax_mm, GROUPS)
                    reach(sp, y_done, g + 1)
                    sp.dma_start(xr[q][:], x_groups[g + 2]).then_inc(x_in[q], 16)

            def piece_keys(g, q):
                if exists(g + 1):
                    r = (q + 1) % 2
                    if isinstance(g, int) and g < 1:
                        sp.wait_ge(k_zeroed, r + 1)
                    sp.wait_ge(k_lo_done, g + 2)
                    reach(sp, s_mm, (g - 1) * GB + GB)
                    for h in range(HEADS):
                        rows = slice(h * HEAD_DIM, (h + 1) * HEAD_DIM)
                        sp.dma_start(k_diag[r][rows, :, h, :].bitcast(F32),
                                     k_parts[r][rows, :, :].bitcast(F32)).then_inc(k_in[r], 16)

            def piece_store(g, q):
                if exists(g - 2):
                    sp.wait_ge(res_done, g - 1)
                    sp.dma_start(out_groups[g - 2], res[q][:]).then_inc(stored[q], 16)

            def body(g, q):
                piece_loads(g, q)
                piece_keys(g, q)
                piece_store(g, q)

            attention_schedule(sp, body, -2)
            for q in range(2):
                sp.wait_ge(stored[q], 16 * GROUPS // 2)

        @block.gpsimd
        def _(pool):
            pool.memset(ident[:], 0.0).then_inc(zeroed, 1)
            pool.wait_ge(zeroed, 1)
            pool.affine_select(out=ident[:], in_=ident[:], compare_op=ALU.not_equal, fill=1.0, base=0,
                               pattern=[[-1, P]], channel_multiplier=1).then_inc(ident_made, 1)

            pool.memset(k_diag[0][:].bitcast(F32), 0.0).then_inc(k_zeroed, 1)
            pool.memset(minus_half[:], -0.5).then_inc(half_made, 1)
            pool.memset(eps[:], EPS).then_inc(half_made, 1)
            pool.wait_ge(half_made, 2)

            def pass1_hi(g, q):
                if not exists(g):
                    return
                pool.wait_ge(hid1_done, g + 1)
                pool.tensor_copy(group_states(state_hi, g), group_states(state, g)).then_inc(hid1_hi_done, 1)

            def pass1_lo(g, q):
                if not exists(g):
                    return
                pool.wait_ge(hid1_hi_done, g + 1)
                pool.tensor_tensor(group_states(state_lo, g), group_states(state, g), group_states(state_hi, g).bitcast(F32),
                                  ALU.subtract).then_inc(pass1_done, 1)

            def graph_body(g, q):
                pass1_hi(g - 4, q)
                pass1_lo(g - 4, q)

            graph_schedule(pool, graph_body)

            def job(j):
                if j.step == 0:
                    return
                c = columns(cell[j.side], j.p)
                pool.wait_ge(gate_done, j.gates + 1)
                pool.tensor_tensor(c, columns(gate[j.turn][GATE_F], j.p), c, ALU.mult).then_inc(kept_done, 1)
                if j.step == j.p - 1 and j.p < MAX_SKIP:
                    full, hi, lo = (window(s, j) for s in (state, state_hi, state_lo))
                    pool.wait_ge(hid_done, j.number + 1)
                    pool.tensor_copy(hi, full).then_inc(last_hi_done, 1)
                    pool.wait_ge(last_hi_done, j.lasts + 1)
                    pool.tensor_tensor(lo, full, hi.bitcast(F32), ALU.subtract).then_inc(last_split, 1)

            def gather_state(g, q):
                if not exists(g):
                    return
                reach(pool, hgT_mm, g - 1)
                pool.tensor_copy(hg[q][:], state[:, :, bass.ds(g * GB, GB)].rearrange("k t b -> k b t")).then_inc(hg_done, 1)

            def rstd(g, q, mv, mv_done, var, var_done, rstd, rstd_done):
                if not exists(g):
                    return
                pool.wait_ge(mv_done, g + 1)
                pool.tensor_tensor(var[q][:], mv[q][:, :, 1], eps[:], ALU.add).then_inc(var_done, 1)
                pool.wait_ge(var_done, g + 1)
                pool.tensor_tensor(rstd[q][:], var[q][:], minus_half[:], ALU.pow).then_inc(rstd_done, 1)

            def keep_x1(g, q):
                if not exists(g):
                    return
                pool.wait_ge(x1_done, (g + 1) * GB)
                pool.tensor_copy(x1_all[:, bass.ds(g * GB, GB), :], x1[q][:]).then_inc(x1_kept, 1)

            def rstd_1(g, q):
                rstd(g, q, mv1, mv1_done, var1, var1_done, rstd1, rstd1_done)

            def between(n):
                if n == -1:
                    pool.wait_ge(hid_done, START[MAX_SKIP][0] + 2 * (MAX_SKIP - 2) + 1)
                    gather_state(0, 0)
                if n == 0:
                    rstd_1(0, 0)
                    gather_state(1, 1)
                if n == 1:
                    pool.memset(k_diag[1][:].bitcast(F32), 0.0).then_inc(k_zeroed, 1)
                if n == 3:
                    rstd_1(1, 1)
                if n == 4:
                    gather_state(2, 0)

            lstm_schedule(pool, job, between)

            pool.wait_ge(hid_done, ALL_JOBS)
            keep_x1(0, 0)

            def body(g, q):
                gather_state(after_first(g) + 1, q)
                rstd(g - 2, q, mv2, mv2_done, var2, var2_done, rstd2, rstd2_done)
                rstd_1(g + 2, q)
                keep_x1(g + 1, (q + 1) % 2)

            attention_schedule(pool, body, 0)

        @block.tensor
        def _(pe):
            pe.wait_ge(ident_made, 1)
            pe.wait_ge(adj_in, 16)
            pe.transpose(bank[:, 0, 0:P], adj_nat[:], ident[:]).then_inc(prep_pe, 1)
            pe.wait_ge(adjT_done, 1)

            def product(out_bank, hi, lo, x_hi, x_lo, first, last):
                pe.matmul(out_bank, lo, x_hi, start=first, stop=False)
                pe.matmul(out_bank, hi, x_lo, start=False, stop=False)
                return pe.matmul(out_bank, hi, x_hi, start=False, stop=last)

            def adj_x(g, q):
                if not exists(g):
                    return
                pe.wait_ge(x_in[q], g * 8 + (16 - 8 * q))
                reach(pe, ax_copied, g)
                for b in range(GB):
                    mm = pe.matmul(bank[:, AX_BANK, b * P:(b + 1) * P], xr[q][:, b, :], adjT[:], start=True, stop=True)
                mm.then_inc(ax_mm, 1)

            def adj_h(g, q):
                if not exists(g):
                    return
                pe.wait_ge(h0_done, g + 1)
                reach(pe, ah_lo_done, g)
                for b in range(GB):
                    mm = pe.matmul(bank[:, AH_BANK, b * P:(b + 1) * P], h0[q][:, b, :], adjT[:], start=True, stop=True)
                mm.then_inc(ah_mm, 1)

            def times_wg0(g, q):
                if not exists(g):
                    return
                pe.wait_ge(ax_copied, g + 1)
                reach(pe, pre0_done, g)
                for b in range(GB):
                    mm = pe.matmul(bank[:, XW_BANK, b * P:(b + 1) * P], ax[q][:, b * P:(b + 1) * P], wg0[:], start=True, stop=True)
                mm.then_inc(xw_mm, 1)

            def times_wg1(g, q):
                if not exists(g):
                    return
                if isinstance(g, int) and g == 0:
                    pe.wait_ge(wg1_lo_done, 1)
                pe.wait_ge(ah_lo_done, g + 1)
                reach(pe, pre1_done, g)
                product(bank[:, HW_BANK, :], wg1_hi[:], wg1_lo[:], ah_hi[q][:], ah_lo[q][:], True, True).then_inc(hw_mm, 1)

            def pass1_gates(g, q):
                if not exists(g):
                    return
                if isinstance(g, int) and g == 0:
                    pe.wait_ge(w_lo_done, QUADS)
                    pe.wait_ge(bias_done, 1)
                pe.wait_ge(lo1_done, g + 1)
                reach(pe, gate1_done, g * 3)
                for n, k in enumerate(gates_of(0)):
                    product(bank[:, GATE1_BANK[n], :], wih_hi[0][:, k, :], wih_lo[0][:, k, :], h1_hi[q][:], h1_lo[q][:], True,
                            True).then_inc(gate1_mm, 1)

            def turn_weights(g):
                if isinstance(g, int) and g == 0:
                    pe.wait_ge(gcn_weights_in, 64)
                    for bias_bank, left, right in ((BIAS_BANK[0], adjT, bg0_rows), (BIAS_BANK[1], bg1_rows, adjT)):
                        pe.matmul(bank[:, bias_bank, 0:P], left[:], right[:], start=True, stop=True).then_inc(prep_pe, 1)
                for n in weight_quads(g):
                    raw, p = quads[n][0], quads[n][3]
                    if n == 0:
                        pe.wait_ge(prep_dve, 2)
                        pe.wait_ge(wih_in, 16)
                        pe.wait_ge(bias_sum, 1)
                        pe.transpose(bank[:, W_BANK[0], 0:4 * MAX_SKIP], b_sum[:],
                                     ident[0:4 * MAX_SKIP, 0:4 * MAX_SKIP]).then_inc(bias_mm, 1)
                        pe.wait_ge(bias_done, 1)
                    if n == MAX_SKIP:
                        pe.wait_ge(whh_in, 16)
                    reach(pe, w_lo_done, n - 3)
                    for k in QUARTERS:
                        mm = pe.transpose(bank[:, W_BANK[n % 4], k * P:(k + 1) * P], raw[:, p, k, :], ident[:])
                    mm.then_inc(wT_mm, 1)

            def graph_body(g, q):
                r = (q + 1) % 2
                adj_x(g, q)
                times_wg1(g - 2, q)
                turn_weights(g)
                pass1_gates(g - 3, r)
                adj_h(g - 1, r)
                times_wg0(g, q)

            graph_schedule(pe, graph_body)

            def job(j):
                p = j.p
                whole = isinstance(j.number, int)
                if whole and j.number == 0:
                    pe.wait_ge(pass1_done, 4)
                    pe.wait_ge(pre1_done, GROUPS)
                if p == 2 and j.step == 0 and not (whole and j.number < 2) and j.side == 0:
                    pe.wait_ge(pass1_done, (j.pair + 1) * (2 * CHUNK[2] // GB))
                if not (whole and j.number < 2) and not j.shared:
                    pe.wait_ge(gate_done, j.gates - j.gates_of_last)
                if p > 2 and j.step == 0 and j.side == 0:
                    pairs = CHUNK[p] // CHUNK[p - 1]
                    pe.wait_ge(last_split, j.pair * (2 * pairs) + (START[p - 1][3] + 2 * pairs))
                x_hi, x_lo = (window(s, j) for s in (state_hi, state_lo))
                gates = gates_of(j.step)
                outs = {k: columns(bank[:, j.banks + k, :], p) for k in gates}
                for n, k in enumerate(gates):
                    if whole and j.number == 1 and 4 + k in GATE1_BANK:
                        pe.wait_ge(gate1_done, 3 * (GROUPS - 1) + GATE1_BANK.index(4 + k) + 1)
                    if whole and j.number == ALL_JOBS - 5 and k == FIRST_HG_BANK - 4:
                        pe.wait_ge(y_done, 1)
                    if j.shared:
                        pe.wait_ge(gate_done, j.gates - j.gates_of_last + n + 1)
                    mm = product(outs[k], wih_hi[p - 1][:, k, :], wih_lo[p - 1][:, k, :], x_hi, x_lo, True, j.step == 0)
                    if j.step == 0:
                        mm.then_inc(gate_mm, 1)
                if j.step > 0:
                    pe.wait_ge(hid_split, j.before)
                    h_hi, h_lo = (columns(s[j.side], p) for s in (hid_hi, hid_lo))
                    for k in gates:
                        product(outs[k], whh_hi[p - 2][:, k, :], whh_lo[p - 2][:, k, :], h_hi, h_lo, False,
                                True).then_inc(gate_mm, 1)

            def piece_hgT(g, q, to=HG_BANK):
                if not exists(g):
                    return
                pe.wait_ge(hg_done, g + 1)
                reach(pe, x1T_done, g)
                for b in range(GB):
                    mm = pe.transpose(bank[:, to, b * P:(b + 1) * P], hg[q][:, b, :], ident[:])
                mm.then_inc(hgT_mm, 1)

            def piece_x1T(g, q):
                if not exists(g):
                    return
                pe.wait_ge(x1_done, (g + 1) * GB)
                for b in range(GB):
                    mm = pe.transpose(bank[:, HG_BANK, b * P:(b + 1) * P], x1[q][:, b, :], ident[:])
                mm.then_inc(x1T_mm, 1)

            def piece_k(g, q):
                if not exists(g):
                    return
                if isinstance(g, int) and g == 0:
                    pe.wait_ge(qkv_weights_in, 16)
                pe.wait_ge(x1T_done, g + 1)
                reach(pe, scaled_done, g - 2)
                pe.matmul(bank[:, K_BANK, :], wqkv[:, DIM:2 * DIM], x1T[q][:], start=True, stop=True).then_inc(k_mm, 1)

            def piece_q(g, q):
                if not exists(g):
                    return
                reach(pe, v_done, g)
                pe.matmul(bank[:, Q_BANK, :], wqkv[:, 0:DIM], x1T[q][:], start=True, stop=True).then_inc(q_mm, 1)

            def piece_v(g, q):
                if not exists(g):
                    return
                pe.wait_ge(q_lo_done, g + 1)
                for b in range(GB):
                    mm = pe.matmul(bank[:, Q_BANK, b * P:(b + 1) * P], x1T[q][:, b * P:(b + 1) * P],
                                   wqkv[:, 2 * DIM:3 * DIM], start=True, stop=True)
                mm.then_inc(v_mm, 1)

            def piece_o(g, q):
                if not exists(g):
                    return
                pe.wait_ge(oT_done, g + 1)
                reach(pe, scaled_done, g)
                reach(pe, k_lo_done, g + 3 if not isinstance(g, int) else min(g + 3, GROUPS))
                for b in range(GB):
                    mm = pe.transpose(bank[:, K_BANK, b * P:(b + 1) * P], oT[q][:, b * P:(b + 1) * P], ident[:])
                mm.then_inc(o_mm, 1)

            def scores(g, q, b):
                if not exists(g):
                    return
                n = g * GB + b
                if b == 0:
                    pe.wait_ge(k_in[q], g * 32 + (64 - 32 * q))
                reach(pe, exp_done, n - 1)
                if isinstance(g, int) and g == 0 and b == 0:
                    pe.wait_ge(gate_done, ALL_GATES - 2)
                    pe.wait_ge(mask_made, 1)
                    pe.wait_ge(ident_bf_made, 1)
                out_bank = bank[:, S_BANK[b % 2], :].rearrange("i (h j) -> i h j", h=HEADS)
                pe.matmul(out_bank, ident_bf[:], mask[:].to_broadcast([P, HEADS, P]), start=True, stop=False)
                tokens = slice(b * P, (b + 1) * P)
                product(out_bank, q_hi[q][:, tokens], q_lo[q][:, tokens], k_diag[q][:, b, :, :], k_diag[q][:, GB + b, :, :],
                        False, True).then_inc(s_mm, 1)

            def turn_probs(g, b):
                if not exists(g):
                    return
                n = g * GB + b
                pe.wait_ge(exp_done, n + 1)
                reach(pe, pT_done, n - 1)
                for h in range(HEADS):
                    mm = pe.transpose(bank[:, PT_BANK[b % 2], h * P:(h + 1) * P], probs[b % 2][:, h, :], ident[:])
                mm.then_inc(pT_mm, 1)

            def values(g, q, b):
                if not exists(g):
                    return
                n = g * GB + b
                pe.wait_ge(pT_done, n + 1)
                if b == 0:
                    pe.wait_ge(v_done, g + 1)
                    reach(pe, oT_done, g)
                for h in range(HEADS):
                    rows = slice(h * HEAD_DIM, (h + 1) * HEAD_DIM)
                    mm = pe.matmul(bank[rows, O_BANK, b * P:(b + 1) * P], v[q][:, b, rows], probsT[b % 2][:, h, :],
                                   start=True, stop=True)
                mm.then_inc(pv_mm, 1)

            def between(n):
                if n == -1:
                    piece_hgT(0, 0, FIRST_HG_BANK)
                if n == 1:
                    pe.wait_ge(gate_done, ALL_GATES - 5 * 4)
                    piece_x1T(0, 0)
                if n == 2:
                    piece_hgT(1, 1)
                    piece_k(0, 0)
                    piece_q(0, 0)
                if n == 3:
                    piece_v(0, 0)
                if n == 4:
                    piece_x1T(1, 1)

            lstm_schedule(pe, job, between)

            def body(g, q):
                r = (q + 1) % 2
                scores(g, q, 0)
                values(g - 1, r, 1)
                turn_probs(g - 1, 2)
                piece_x1T(after_first(g), r)
                scores(g, q, 1)
                turn_probs(g - 1, 3)
                piece_k(g + 1, r)
                piece_hgT(g + 2, q)
                piece_q(g + 1, r)
                values(g - 1, r, 2)
                scores(g, q, 2)
                turn_probs(g, 0)
                values(g - 1, r, 3)
                scores(g, q, 3)
                turn_probs(g, 1)
                piece_v(g + 1, r)
                values(g, q, 0)
                piece_o(g - 1, r)

            attention_schedule(pe, body, 0)

        @block.scalar
        def _(act):
            act.dma_start(wg0[:], Wg0).then_inc(gcn_weights_in, 16)
            act.dma_start(wg1[:], Wg1).then_inc(gcn_weights_in, 16)
            act.dma_start(b_raw[:, 0, :], bih.rearrange("p (q r) -> (p q) r", r=P)).then_inc(lstm_biases_in, 16)
            act.dma_start(b_raw[:, 1, :], bhh.rearrange("p (q r) -> (p q) r", r=P)).then_inc(lstm_biases_in, 16)
            act.wait_ge(ident_made, 1)
            act.copy(ident_bf[:], ident[:]).then_inc(ident_bf_made, 1)
            act.wait_ge(gcn_weights_in, 64)
            act.copy(wg1_hi[:], wg1[:]).then_inc(wg1_hi_done, 1)

            def copy_ax(g, q):
                if not exists(g):
                    return
                act.wait_ge(ax_mm, g + 1)
                reach(act, xw_mm, g - 1)
                act.copy(ax[q][:], bank[:, AX_BANK, :]).then_inc(ax_copied, 1)

            def relu0(g, q):
                if not exists(g):
                    return
                act.wait_ge(pre0_done, g + 1)
                reach(act, ah_mm, g - 1)
                act.activation(h0[q][:], pre0[q][:], ACT.Relu).then_inc(h0_done, 1)

            def high_ah(g, q):
                if not exists(g):
                    return
                act.wait_ge(ah_mm, g + 1)
                reach(act, hw_mm, g - 1)
                act.copy(ah_hi[q][:], bank[:, AH_BANK, :]).then_inc(ah_hi_done, 1)

            def relu1(g, q):
                if not exists(g):
                    return
                act.wait_ge(pre1_done, g + 1)
                reach(act, gate1_mm, (g - 1) * 3)
                act.activation(h1_hi[q][:], pre1[q][:], ACT.Relu).then_inc(hi1_done, 1)

            def pass1_gates(g, q):
                if not exists(g):
                    return
                for n, k in enumerate(gates_of(0)):
                    act.wait_ge(gate1_mm, g * 3 + (n + 1))
                    act.activation(gate1[q][n][:], bank[:, GATE1_BANK[n], :], GATE_FUNCTION[k],
                                   bias=gate_bias[:, k:k + 1]).then_inc(gate1_done, 1)

            def pass1_tanh(g, q):
                if not exists(g):
                    return
                act.wait_ge(cell1_done, g + 1)
                act.activation(cell1_tanh[q][:], cell1[q][:], ACT.Tanh).then_inc(tanh1_done, 1)

            def split_weights(g):
                for n in weight_quads(g):
                    hi, p = quads[n][1], quads[n][3]
                    if n == 0:
                        act.wait_ge(bias_mm, 1)
                        act.copy(gate_bias[:], bank[:, W_BANK[0], 0:4 * MAX_SKIP]).then_inc(bias_done, 1)
                        act.wait_ge(bias_done, 1)
                    act.wait_ge(wT_mm, n + 1)
                    act.copy(hi[p][:], bank[:, W_BANK[n % 4], :].rearrange("k (q r) -> k q r", q=4)).then_inc(w_hi_done, 1)

            def graph_body(g, q):
                r = (q + 1) % 2
                split_weights(g)
                copy_ax(g, q)
                pass1_gates(g - 3, r)
                high_ah(g - 1, r)
                relu1(g - 2, q)
                pass1_tanh(g - 3, r)
                relu0(g, q)

            graph_schedule(act, graph_body)

            def job(j):
                p = j.p
                if not (isinstance(j.number, int) and j.number < 2):
                    act.wait_ge(hid_done, j.number - 1)
                for n, k in enumerate(gates_of(j.step)):
                    act.wait_ge(gate_mm, j.gates + (n + 1))
                    act.activation(columns(gate[j.turn][k], p), columns(bank[:, j.banks + k, :], p), GATE_FUNCTION[k],
                                   bias=gate_bias[:, 4 * (p - 1) + k:4 * (p - 1) + k + 1]).then_inc(gate_done, 1)
                act.wait_ge(cell_done, j.number + 1)
                act.activation(columns(cell_tanh[j.turn], p), columns(cell[j.side], p), ACT.Tanh).then_inc(tanh_done, 1)

            def copy_x1T(g, q):
                if not exists(g):
                    return
                act.wait_ge(x1T_mm, g + 1)
                reach(act, v_mm, g - 1)
                act.copy(x1T[q][:], bank[:, HG_BANK, :]).then_inc(x1T_done, 1)

            def high_k(g, q):
                if not exists(g):
                    return
                act.wait_ge(k_mm, g + 1)
                reach(act, k_in[q], g * 32 - 32 * q)
                act.copy(k_parts[q][:, 0:GB, :], bank[:, K_BANK, :].rearrange("k (b t) -> k b t", b=GB)).then_inc(k_hi_done, 1)

            def high_q(g, q):
                if not exists(g):
                    return
                act.wait_ge(q_mm, g + 1)
                reach(act, s_mm, (g - 1) * GB)
                act.mul(q_hi[q][:], bank[:, Q_BANK, :], HEAD_DIM ** -0.5).then_inc(q_hi_done, 1)

            def copy_v(g, q):
                if not exists(g):
                    return
                act.wait_ge(v_mm, g + 1)
                reach(act, pv_mm, (g - 1) * GB)
                act.copy(v[q][:], bank[:, Q_BANK, :].rearrange("t (b d) -> t b d", b=GB)).then_inc(v_done, 1)

            def copy_oT(g, q):
                if not exists(g):
                    return
                act.wait_ge(pv_mm, (g + 1) * GB)
                act.copy(oT[q][:], bank[:, O_BANK, :]).then_inc(oT_done, 1)

            def exponentials(g, q, b):
                if not exists(g):
                    return
                n = g * GB + b
                act.wait_ge(max_done, n + 1)
                reach(act, pT_mm, n - 1)
                if b == 0:
                    reach(act, rden_done, g - 1)
                for h in range(HEADS):
                    e = act.activation(probs[b % 2][:, h, :], bank[:, S_BANK[b % 2], h * P:(h + 1) * P], ACT.Exp,
                                       bias=neg_max[b % 2][:, h:h + 1], accum_out=den[q][:, b * HEADS + h:b * HEADS + h + 1])
                e.then_inc(exp_done, 1)

            def copy_pT(g, b):
                if not exists(g):
                    return
                n = g * GB + b
                act.wait_ge(pT_mm, n + 1)
                reach(act, pv_mm, n - 1)
                act.copy(probsT[b % 2][:], bank[:, PT_BANK[b % 2], :].rearrange("j (h i) -> j h i", h=HEADS)).then_inc(pT_done, 1)

            def between(n):
                if n == 1:
                    copy_x1T(0, 0)
                if n == 2:
                    high_k(0, 0)
                    high_q(0, 0)
                if n == 4:
                    copy_x1T(1, 1)

            lstm_schedule(act, job, between)
            act.wait_ge(half_made, 2)
            act.activation(exp_eps[:], eps[:], ACT.Exp)

            def body(g, q):
                r = (q + 1) % 2
                copy_v(g, q)
                copy_pT(g - 1, 2)
                copy_x1T(after_first(g), r)
                exponentials(g, q, 0)
                high_k(g + 1, r)
                copy_pT(g - 1, 3)
                exponentials(g, q, 1)
                high_q(g + 1, r)
                copy_pT(g, 0)
                copy_oT(g - 1, r)
                exponentials(g, q, 2)
                copy_pT(g, 1)
                exponentials(g, q, 3)

            attention_schedule(act, body, 0)

        @block.vector
        def _(dve):
            dve.wait_ge(adj_in, 16)
            dve.tensor_scalar(mask[:, 0, :], adj_nat[:], 0.0, MASKED, ALU.is_equal, ALU.mult).then_inc(mask_made, 1)
            dve.wait_ge(prep_pe, 1)
            dve.tensor_copy(adjT[:], bank[:, 0, 0:P]).then_inc(adjT_done, 1)
            dve.wait_ge(prep_pe, 3)
            dve.tensor_copy(bias0[:, 0, :], bank[:, BIAS_BANK[0], 0:P]).then_inc(prep_dve, 1)
            dve.tensor_copy(bias1[:, 0, :], bank[:, BIAS_BANK[1], 0:P]).then_inc(prep_dve, 1)
            dve.wait_ge(wg1_hi_done, 1)
            dve.tensor_tensor(wg1_lo[:], wg1[:], wg1_hi[:].bitcast(F32), ALU.subtract).then_inc(wg1_lo_done, 1)
            dve.wait_ge(prep_dve, 2)
            dve.wait_ge(lstm_biases_in, 16 * 2)
            dve.tensor_tensor(b_sum[:], b_raw[:, 0, :], b_raw[:, 1, :], ALU.add).then_inc(bias_sum, 1)

            def add0(g, q):
                if not exists(g):
                    return
                dve.wait_ge(xw_mm, g + 1)
                reach(dve, h0_done, g - 1)
                dve.tensor_tensor(pre0[q][:], bank[:, XW_BANK, :].rearrange("t (b d) -> t b d", b=GB),
                                  bias0[:].to_broadcast([P, GB, DIM]), ALU.add).then_inc(pre0_done, 1)

            def low_ah(g, q):
                if not exists(g):
                    return
                dve.wait_ge(ah_hi_done, g + 1)
                dve.tensor_tensor(ah_lo[q][:], bank[:, AH_BANK, :], ah_hi[q][:].bitcast(F32), ALU.subtract).then_inc(ah_lo_done, 1)

            def add1(g, q):
                if not exists(g):
                    return
                dve.wait_ge(hw_mm, g + 1)
                reach(dve, lo1_done, g - 1)
                dve.tensor_tensor(pre1[q][:].rearrange("k (b t) -> k b t", b=GB),
                                  bank[:, HW_BANK, :].rearrange("k (b t) -> k b t", b=GB),
                                  bias1[:].to_broadcast([P, GB, STEPS]), ALU.add).then_inc(pre1_done, 1)

            def low1(g, q):
                if not exists(g):
                    return
                dve.wait_ge(hi1_done, g + 1)
                dve.scalar_tensor_tensor(out=h1_lo[q][:], in0=pre1[q][:], scalar=0.0, in1=h1_hi[q][:].bitcast(F32),
                                         op0=ALU.max, op1=ALU.subtract).then_inc(lo1_done, 1)

            def pass1_cell(g, q):
                if not exists(g):
                    return
                dve.wait_ge(gate1_done, g * 3 + 2)
                dve.tensor_tensor(cell1[q][:], gate1[q][0][:], gate1[q][1][:], ALU.mult).then_inc(cell1_done, 1)

            def pass1_hidden(g, q):
                if not exists(g):
                    return
                dve.wait_ge(tanh1_done, g + 1)
                dve.wait_ge(gate1_done, g * 3 + 3)
                dve.tensor_tensor(group_states(state, g), gate1[q][2][:].rearrange("k (b t) -> k b t", b=GB),
                                  cell1_tanh[q][:].rearrange("k (b t) -> k b t", b=GB), ALU.mult).then_inc(hid1_done, 1)

            def split_weights(g):
                for n in weight_quads(g):
                    _, hi, lo, p = quads[n]
                    dve.wait_ge(w_hi_done, n + 1)
                    dve.tensor_tensor(lo[p][:], bank[:, W_BANK[n % 4], :].rearrange("k (q r) -> k q r", q=4),
                                      hi[p][:].bitcast(F32), ALU.subtract).then_inc(w_lo_done, 1)

            def graph_body(g, q):
                r = (q + 1) % 2
                add1(g - 2, q)
                split_weights(g)
                pass1_cell(g - 3, r)
                low_ah(g - 1, r)
                low1(g - 2, q)
                add0(g, q)
                pass1_hidden(g - 3, r)

            graph_schedule(dve, graph_body)

            def job(j):
                p = j.p
                i_, _, g_, o_ = (columns(gate[j.turn][k], p) for k in QUARTERS)
                c = columns(cell[j.side], p)
                if j.step == 0:
                    dve.wait_ge(gate_done, j.gates + 2)
                    dve.tensor_tensor(c, i_, g_, ALU.mult).then_inc(cell_done, 1)
                else:
                    new = columns(in_cell[j.turn], p)
                    dve.wait_ge(gate_done, j.gates + 3)
                    dve.tensor_tensor(new, i_, g_, ALU.mult).then_inc(in_cell_done, 1)
                    dve.wait_ge(in_cell_done, j.later + 1)
                    dve.wait_ge(kept_done, j.later + 1)
                    dve.tensor_tensor(c, c, new, ALU.add).then_inc(cell_done, 1)
                full, hi, lo = (columns(s[j.side], p) for s in (hid, hid_hi, hid_lo))
                if j.step == p - 1:
                    full = window(state, j)
                dve.wait_ge(tanh_done, j.number + 1)
                dve.tensor_tensor(full, o_, columns(cell_tanh[j.turn], p), ALU.mult).then_inc(hid_done, 1)
                if j.step == p - 1:
                    return
                dve.wait_ge(hid_done, j.number + 1)
                dve.tensor_copy(hi, full).then_inc(hid_hi_done, 1)
                dve.wait_ge(hid_hi_done, j.split + 1)
                dve.tensor_tensor(lo, full, hi.bitcast(F32), ALU.subtract).then_inc(hid_split, 1)

            def maximum(g, b):
                if not exists(g):
                    return
                n = g * GB + b
                dve.wait_ge(s_mm, n + 1)
                reach(dve, exp_done, n - 1)
                dve.tensor_reduce(neg_max[b % 2][:], bank[:, S_BANK[b % 2], :].rearrange("i (h j) -> i h j", h=HEADS),
                                  AX_X, ALU.max, negate=True).then_inc(max_done, 1)

            def partial_stats(source, stats, bn_done):
                for b in range(GB):
                    last = dve.bn_stats(stats[:, b, :], source[:, b, :])
                last.then_inc(bn_done, 1)

            def mean_var(g, stats, mv, mv_done):
                if not exists(g):
                    return
                for b in range(GB):
                    last = dve.bn_aggr(mv[:, b, :], stats[:, b, :])
                last.then_inc(mv_done, 1)

            def stats_ready(g, bn_done):
                if exists(g):
                    dve.wait_ge(bn_done, g + 1)

            def residual1(g, q, source=HG_BANK):
                if not exists(g):
                    return
                dve.wait_ge(hgT_mm, g + 1)
                dve.wait_ge(x_in[q], g * 8 + (16 - 8 * q) + 16 * (GROUPS // 2))
                reach(dve, x1_done, (g - 1) * GB)
                dve.tensor_tensor(y[q][:], bank[:, source, :].rearrange("t (b d) -> t b d", b=GB), xr[q][:],
                                  ALU.add).then_inc(y_done, 1)
                dve.wait_ge(y_done, g + 1)
                partial_stats(y[q], stats1[q], bn1_done)

            def norm1(g, q):
                if not exists(g):
                    return
                dve.wait_ge(rstd1_done, g + 1)
                reach(dve, x1_kept, g - 1)
                reach(dve, x1T_mm, g - 1)
                for b in range(GB):
                    dve.tensor_scalar(x1[q][:, b, :], y[q][:, b, :], mv1[q][:, b, 0:1], rstd1[q][:, b:b + 1],
                                      ALU.subtract, ALU.mult).then_inc(x1_done, 1)

            def low_k(g, q):
                if not exists(g):
                    return
                dve.wait_ge(k_hi_done, g + 1)
                dve.tensor_tensor(k_parts[q][:, GB:2 * GB, :], bank[:, K_BANK, :].rearrange("k (b t) -> k b t", b=GB),
                                  k_parts[q][:, 0:GB, :].bitcast(F32), ALU.subtract).then_inc(k_lo_done, 1)

            def low_q(g, q):
                if not exists(g):
                    return
                dve.wait_ge(q_hi_done, g + 1)
                dve.scalar_tensor_tensor(out=q_lo[q][:], in0=bank[:, Q_BANK, :], scalar=HEAD_DIM ** -0.5,
                                         in1=q_hi[q][:].bitcast(F32), op0=ALU.mult, op1=ALU.subtract).then_inc(q_lo_done, 1)

            def reciprocal(g, q):
                if not exists(g):
                    return
                dve.wait_ge(exp_done, (g + 1) * GB)
                dve.reciprocal(rden[q][:, :, 0], den[q][:]).then_inc(rden_done, 1)

            def residual2(g, q):
                if not exists(g):
                    return
                dve.wait_ge(o_mm, g + 1)
                dve.wait_ge(rden_done, g + 1)
                dve.tensor_tensor(z[q][:].rearrange("t b (h d) -> t (b h) d", h=HEADS),
                                  bank[:, K_BANK, :].rearrange("t (c d) -> t c d", d=HEAD_DIM),
                                  rden[q][:].to_broadcast([P, GB * HEADS, HEAD_DIM]), ALU.mult).then_inc(scaled_done, 1)
                dve.wait_ge(scaled_done, g + 1)
                dve.wait_ge(x1_kept, g + 1)
                dve.tensor_tensor(z[q][:], z[q][:], x1_all[:, bass.ds(g * GB, GB), :], ALU.add).then_inc(z_done, 1)
                dve.wait_ge(z_done, g + 1)
                partial_stats(z[q], stats2[q], bn2_done)

            def norm2(g, q):
                if not exists(g):
                    return
                dve.wait_ge(rstd2_done, g + 1)
                reach(dve, stored[q], g * 8 - 8 * q)
                for b in range(GB):
                    last = dve.tensor_scalar(res[q][:, b, :], z[q][:, b, :], mv2[q][:, b, 0:1], rstd2[q][:, b:b + 1],
                                             ALU.subtract, ALU.mult)
                last.then_inc(res_done, 1)

            def between(n):
                if n == -1:
                    residual1(0, 0, FIRST_HG_BANK)
                    dve.wait_ge(bn1_done, 1)
                    mean_var(0, stats1[0], mv1[0], mv1_done)
                if n == 0:
                    norm1(0, 0)
                if n == 2:
                    residual1(1, 1)
                    dve.wait_ge(bn1_done, 2)
                    mean_var(1, stats1[1], mv1[1], mv1_done)
                    low_k(0, 0)
                    low_q(0, 0)
                if n == 3:
                    norm1(1, 1)

            lstm_schedule(dve, job, between)

            def body(g, q):
                r = (q + 1) % 2
                maximum(g, 0)
                residual2(g - 2, q)
                reciprocal(g - 1, r)
                stats_ready(g - 2, bn2_done)
                maximum(g, 1)
                mean_var(g - 2, stats2[q], mv2[q], mv2_done)
                low_k(g + 1, r)
                residual1(g + 2, q)
                maximum(g, 2)
                low_q(g + 1, r)
                stats_ready(g + 2, bn1_done)
                maximum(g, 3)
                mean_var(g + 2, stats1[q], mv1[q], mv1_done)
                norm2(g - 2, q)
                norm1(g + 2, q)

            attention_schedule(dve, body, 0)


_INPUTS = ("x", "adj", "L0_gnn_Wg0", "L0_gnn_bg0", "L0_gnn_Wg1", "L0_gnn_bg1", "L0_gnn_Wih", "L0_gnn_Whh",
           "L0_gnn_bih", "L0_gnn_bhh", "L1_gnn_W")


def kernel(**inputs):
    import numpy as np
    import concourse.bacc as bacc
    from concourse.bass_utils import run_bass_kernel_spmd

    nc = bacc.Bacc("TRN2", target_bir_lowering=False, num_devices=1)
    arrays, args = {}, []
    for name in _INPUTS:
        a = np.ascontiguousarray(inputs[name])
        arrays[f"in_{name}"] = a
        args.append(nc.dram_tensor(f"in_{name}", a.shape, mybir.dt.from_np(a.dtype), kind="ExternalInput").ap())
    args.append(nc.dram_tensor("out_dram", (BATCH, STEPS, DIM), F32, kind="ExternalOutput").ap())
    build(nc, *args)
    done = run_bass_kernel_spmd(nc, [arrays], core_ids=[0])
    return done.results[0]["out_dram"]
```
